# Optimizing a Trainium2 kernel written in Bass

```python
import numpy as np
import jax
import jax.numpy as jnp

def _softmax(x, axis=-1):
    return jax.nn.softmax(x, axis=axis)

def _gelu(x):
    return jax.nn.gelu(x, approximate=True)

def _silu(x):
    return jax.nn.silu(x)

def _sigmoid(x):
    return jax.nn.sigmoid(x)

def _layernorm(x, axis=-1, eps=1e-05):
    m = jnp.mean(x, axis=axis, keepdims=True)
    v = jnp.var(x, axis=axis, keepdims=True)
    return (x - m) / jnp.sqrt(v + eps)

def _scatter_add(tgt, idx, src, axis=0):
    return tgt.at[idx].add(src)

def _segment_sum(src, seg, n):
    return jax.ops.segment_sum(src, seg, n)
kernel_name = 'mk_decoder_preln_d1_seqx_r8_bd9082'

def setup_inputs(seed: int=0):
    np.random.seed(seed)
    _w = jnp.asarray

    def _rec_inputs():
        import jax
        import jax.numpy as jnp
        _rk = jax.random.key(seed)
        x = 7.22e-05 + 1 * jax.random.normal(jax.random.fold_in(_rk, 1), (2, 512, 128), jnp.float32)
        _lenS = 512 - jax.random.randint(jax.random.fold_in(_rk, 7), (2,), 0, max(1, 512 // 4) + 1, jnp.int32)
        _lenS2 = 77 - jax.random.randint(jax.random.fold_in(_rk, 8), (2,), 0, max(1, 77 // 4) + 1, jnp.int32)
        _ctx_1024P = jax.random.normal(jax.random.fold_in(_rk, 11), (2, 16, 128), jnp.float32)
        _ctx_1024c = jax.random.dirichlet(jax.random.fold_in(_rk, 511), 0.3 * jnp.ones((16,), jnp.float32), (2, 77))
        _ctx_1024t = jnp.einsum('bsk,bkd->bsd', _ctx_1024c, _ctx_1024P)
        _ctx_1024t = _ctx_1024t * jax.lax.rsqrt(jnp.mean(jnp.square(_ctx_1024t)) + 1e-12) * 0.953939
        ctx_1024 = 4.13588e-05 + 0.999923 * (_ctx_1024t + 0.3 * jax.random.normal(jax.random.fold_in(_rk, 611), (2, 77, 128), jnp.float32))
        return (x, ctx_1024)
    x, ctx_1024 = _rec_inputs()

    def _L0_attn_setup():
        import jax, jax.numpy as jnp
        import numpy as np
        EMB, KDIM, B, S = (128, 64, 8, 256)
        key = jax.random.key(seed)
        kx, kq, kk, kv1, kv2 = jax.random.split(key, 5)

        def xavier(k, shape):
            fan_in, fan_out = shape
            lim = (6.0 / (fan_in + fan_out)) ** 0.5
            return jax.random.uniform(k, shape, jnp.float32, -lim, lim)
        return {'x': jax.random.normal(kx, (B, S, EMB), jnp.float32), 'w_q': xavier(kq, (EMB, KDIM)), 'w_k': xavier(kk, (EMB, KDIM)), 'w_v1': xavier(kv1, (EMB, KDIM)), 'w_v2': xavier(kv2, (KDIM, EMB))}
    _L0_attn_all = _L0_attn_setup()
    _L0_attn_in = {k: v for k, v in _L0_attn_all.items() if k in ('w_q', 'w_k', 'w_v1', 'w_v2')}
    del _L0_attn_all

    def _L0_xattn_setup():
        import jax, jax.numpy as jnp
        import numpy as np
        N_EMBD = 128
        COND = 128
        N_HEAD = 16
        B, N, NTOK = (4, 256, 256)
        key = jax.random.key(seed)
        ks = jax.random.split(key, 10)
        s = 0.02
        return {'x': jax.random.normal(ks[0], (B, N, N_EMBD), jnp.float32), 'encoder_output': jax.random.normal(ks[1], (B, NTOK, COND), jnp.float32), 'Wq': jax.random.normal(ks[2], (N_EMBD, N_EMBD), jnp.float32) * s, 'bq': jnp.zeros((N_EMBD,), jnp.float32), 'Wk': jax.random.normal(ks[3], (N_EMBD, COND), jnp.float32) * s, 'bk': jnp.zeros((N_EMBD,), jnp.float32), 'Wv': jax.random.normal(ks[4], (N_EMBD, COND), jnp.float32) * s, 'bv': jnp.zeros((N_EMBD,), jnp.float32), 'Wp': jax.random.normal(ks[5], (N_EMBD, N_EMBD), jnp.float32) * s, 'bp': jnp.zeros((N_EMBD,), jnp.float32)}
    _L0_xattn_all = _L0_xattn_setup()
    _L0_xattn_in = {k: v for k, v in _L0_xattn_all.items() if k in ('Wq', 'bq', 'Wk', 'bk', 'Wv', 'bv', 'Wp', 'bp')}
    del _L0_xattn_all

    def _L0_ffn_setup():
        import jax, jax.numpy as jnp
        import numpy as np
        B, F, D, H, E, K = (4, 256, 128, 256, 8, 2)
        key = jax.random.key(seed)
        ks = jax.random.split(key, 9)
        sc = lambda k, shape, fan_in: jax.random.normal(k, shape, jnp.float32) * fan_in ** (-0.5)
        return {'x': jax.random.normal(ks[0], (B, F, D), jnp.float32), 'rw1': sc(ks[1], (D, D), D), 'rb1': jnp.zeros((D,), jnp.float32), 'rw2': sc(ks[2], (D, E), D), 'rb2': jnp.zeros((E,), jnp.float32), 'ew1': sc(ks[3], (E, D, H), D), 'eb1': jnp.zeros((E, H), jnp.float32), 'ew2': sc(ks[4], (E, H, D), H), 'eb2': jnp.zeros((E, D), jnp.float32)}
    _L0_ffn_all = _L0_ffn_setup()
    _L0_ffn_in = {k: v for k, v in _L0_ffn_all.items() if k in ('rw1', 'rb1', 'rw2', 'rb2', 'ew1', 'eb1', 'ew2', 'eb2')}
    del _L0_ffn_all
    return {'x': x, 'ctx_1024': ctx_1024, 'L0_attn_w_q': _L0_attn_in['w_q'], 'L0_attn_w_k': _L0_attn_in['w_k'], 'L0_attn_w_v1': _L0_attn_in['w_v1'], 'L0_attn_w_v2': _L0_attn_in['w_v2'], 'L0_xattn_Wq': _L0_xattn_in['Wq'], 'L0_xattn_bq': _L0_xattn_in['bq'], 'L0_xattn_Wk': _L0_xattn_in['Wk'], 'L0_xattn_bk': _L0_xattn_in['bk'], 'L0_xattn_Wv': _L0_xattn_in['Wv'], 'L0_xattn_bv': _L0_xattn_in['bv'], 'L0_xattn_Wp': _L0_xattn_in['Wp'], 'L0_xattn_bp': _L0_xattn_in['bp'], 'L0_ffn_rw1': _L0_ffn_in['rw1'], 'L0_ffn_rb1': _L0_ffn_in['rb1'], 'L0_ffn_rw2': _L0_ffn_in['rw2'], 'L0_ffn_rb2': _L0_ffn_in['rb2'], 'L0_ffn_ew1': _L0_ffn_in['ew1'], 'L0_ffn_eb1': _L0_ffn_in['eb1'], 'L0_ffn_ew2': _L0_ffn_in['ew2'], 'L0_ffn_eb2': _L0_ffn_in['eb2']}

def reference(x, ctx_1024, L0_attn_w_q, L0_attn_w_k, L0_attn_w_v1, L0_attn_w_v2, L0_xattn_Wq, L0_xattn_bq, L0_xattn_Wk, L0_xattn_bk, L0_xattn_Wv, L0_xattn_bv, L0_xattn_Wp, L0_xattn_bp, L0_ffn_rw1, L0_ffn_rb1, L0_ffn_rw2, L0_ffn_rb2, L0_ffn_ew1, L0_ffn_eb1, L0_ffn_ew2, L0_ffn_eb2):
    import jax
    import jax.numpy as jnp

    def _L0_attn_ref(x, w_q, w_k, w_v1, w_v2):
        import jax, jax.numpy as jnp
        import numpy as np
        EMB, KDIM, B, S = (128, 64, 8, 256)
        seq = x.shape[1]
        queries = jnp.einsum('bse,ek->bsk', x, w_q)
        keys = jnp.einsum('bse,ek->bsk', x, w_k)
        scale = w_q.shape[1] ** (-0.5)
        scores = jnp.einsum('bqk,bsk->bqs', queries, keys) * scale
        causal = jnp.tril(jnp.ones((seq, seq), dtype=bool))
        scores = jnp.where(causal[None, :, :], scores, -jnp.inf)
        attn = jax.nn.softmax(scores, axis=-1)
        values = jnp.einsum('bsk,ke->bse', jnp.einsum('bse,ek->bsk', x, w_v1), w_v2)
        return jnp.einsum('bqs,bse->bqe', attn, values)

    def _L0_xattn_ref(x, encoder_output, Wq, bq, Wk, bk, Wv, bv, Wp, bp):
        import jax, jax.numpy as jnp
        import numpy as np
        N_EMBD = 128
        COND = 128
        N_HEAD = 16
        B, N, NTOK = (4, 256, 256)
        Bx, Nx, C = x.shape
        H = N_HEAD
        D = C // H
        q = (x @ Wq.T + bq).reshape(Bx, Nx, H, D)
        k = (encoder_output @ Wk.T + bk).reshape(Bx, -1, H, D)
        v = (encoder_output @ Wv.T + bv).reshape(Bx, -1, H, D)
        scale = 1.0 / jnp.sqrt(jnp.asarray(D, x.dtype))
        att = jnp.einsum('bnhd,bthd->bhnt', q, k) * scale
        att = jax.nn.softmax(att, axis=-1)
        y = jnp.einsum('bhnt,bthd->bnhd', att, v).reshape(Bx, Nx, C)
        y = y @ Wp.T + bp
        return y

    def _L0_ffn_ref(x, rw1, rb1, rw2, rb2, ew1, eb1, ew2, eb2):
        import jax, jax.numpy as jnp
        import numpy as np
        B, F, D, H, E, K = (4, 256, 128, 256, 8, 2)
        b, f, d = x.shape
        t = x.reshape(b * f, d)
        logits = jax.nn.silu(t @ rw1 + rb1) @ rw2 + rb2
        vals, idx = jax.lax.top_k(logits, K)
        rows = jnp.arange(t.shape[0])[:, None]
        masked = jnp.full_like(logits, -jnp.inf).at[rows, idx].set(vals)
        w = jax.nn.softmax(masked, axis=1)
        eh = jax.nn.silu(jnp.einsum('td,edh->teh', t, ew1) + eb1[None])
        eo = jnp.einsum('teh,ehd->ted', eh, ew2) + eb2[None]
        y = t + jnp.einsum('te,ted->td', w, eo)
        return y.reshape(b, f, d)
    x = x + _L0_attn_ref(_layernorm(x, axis=-1), L0_attn_w_q, L0_attn_w_k, L0_attn_w_v1, L0_attn_w_v2)
    x = x + _L0_xattn_ref(_layernorm(x, axis=-1), ctx_1024, L0_xattn_Wq, L0_xattn_bq, L0_xattn_Wk, L0_xattn_bk, L0_xattn_Wv, L0_xattn_bv, L0_xattn_Wp, L0_xattn_bp)
    x = x + _L0_ffn_ref(_layernorm(x, axis=-1), L0_ffn_rw1, L0_ffn_rb1, L0_ffn_rw2, L0_ffn_rb2, L0_ffn_ew1, L0_ffn_eb1, L0_ffn_ew2, L0_ffn_eb2)
    return x

_drawn_inputs = setup_inputs


def setup_inputs(seed=0):
    import zlib

    import numpy as np

    out = dict(_drawn_inputs(seed))
    spreads = {'L0_xattn_bq': (0.0, 0.8),
     'L0_xattn_bk': (0.0, 0.8),
     'L0_xattn_bv': (0.0, 0.1),
     'L0_xattn_bp': (0.0, 0.1),
     'L0_ffn_rb1': (0.0, 0.1),
     'L0_ffn_rb2': (0.0, 0.1),
     'L0_ffn_eb1': (0.0, 0.38),
     'L0_ffn_eb2': (0.0, 0.1)}
    factors = {'L0_xattn_Wq': 8.0, 'L0_xattn_Wk': 8.0}
    for name, (base, spread) in spreads.items():
        noise = np.random.default_rng([zlib.crc32(name.encode()), seed]).standard_normal(out[name].shape)
        drawn = base * np.exp(spread * noise) if base else spread * noise
        out[name] = jnp.asarray(drawn.astype(out[name].dtype))
    for name, factor in factors.items():
        out[name] = (out[name] * factor).astype(out[name].dtype)
    return out
```

```python
import concourse.bass as bass
from concourse import mybir

B, S, D = 2, 512, 128
P = 128
NT = S // P
KD = 64
TC = 77
NH, HD = 16, 8
HG = 4
NG = NH // HG
GR = HG * HD
REPS = 3
QR = REPS * GR
MR = 2 * HG
GK = HG * TC
NC = 3
CR = -(-GK // NC)
CROWS = [min(CR, GK - c * CR) for c in range(NC)]
NE, FH, TOPK = 8, 256, 2
FC = FH // P
NU = NE * FC
EPS = 1e-5
MASKED = -3.0e38
NZ = 3
NS = 4

C_ID, C_CAUSAL, C_HMASK, C_VMASK, C_IOTA = 0, 128, 256, 260, 272
C_END = 280
X_WQ, X_WK, X_WV, X_WP = 0, 384, 768, 896
X_BQ, X_BV, X_BP, X_END = 1024, 1028, 1156, 1284
F_RW1, F_RW2, F_RB1, F_EB1, F_RB2, F_END = 0, 128, 136, 137, 153, 161


def decoder_block(nc, x, ctx, consts, self_w, cross_w, bk_row, ffn_w, eb2, ew1, ew2, out):
    f32, f32r, bf16, u32, i32 = (mybir.dt.float32, mybir.dt.float32r, mybir.dt.bfloat16,
                                 mybir.dt.uint32, mybir.dt.int32)
    ALU, ACT, AX = mybir.AluOpType, mybir.ActivationFunctionType, mybir.AxisListType

    def sb(name, shape, dt=f32):
        return nc.alloc_sbuf_tensor(name, shape, dt)

    def sem(name):
        return nc.alloc_semaphore(name)

    def r(ap):
        return ap.bitcast(f32r)

    x_sb = sb("x_sb", [P, B * NT, D])
    cst = sb("cst", [P, C_END])
    ident = cst[:, C_ID:C_ID + P]
    ident_b = sb("ident_b", [P, P], bf16)
    causal_b = sb("causal_b", [P, P], bf16)
    selfw = sb("selfw", [KD, 4 * P])
    crossw = sb("crossw", [P, X_END])
    bkrow = sb("bkrow", [1, NG * QR + TC])
    ffnw = sb("ffnw", [P, F_END])
    eb2_sb = sb("eb2_sb", [NE, D])
    ctx_sb = sb("ctx_sb", [TC, B, D])
    w1_sb = sb("w1_sb", [P, NE, FH])
    w2_sb = sb("w2_sb", [P, NE, FC, D])
    w1_hi = sb("w1_hi", [P, NE, FH])
    w1_lo = sb("w1_lo", [P, NE, FH])
    stats = sb("stats", [P, 3, B, NT, 6])
    meanvar = sb("meanvar", [P, 3, B, NT, 2])
    rs_v = sb("rs_v", [P, 3, B, NT])
    rs_i = sb("rs_i", [P, 3, B, NT], i32)
    rs_y = sb("rs_y", [P, 3, B, 4, NT], i32)
    rs_t = sb("rs_t", [P, 3, B, 6, NT])
    xn = sb("xn", [P, 3, NT, D])
    a_sb = sb("a_sb", [P, P])
    w12 = sb("w12", [P, P])
    xT = [sb(f"xT{b}", [P, S]) for b in range(B)]
    gT = [sb(f"gT{b}", [P, S]) for b in range(B)]
    val = [sb(f"val{b}", [P, NT, D]) for b in range(B)]
    negmax = sb("negmax", [P, B, NT])
    rowsum = sb("rowsum", [P, B, NT])
    rowinv = sb("rowinv", [P, B, NT])
    prob = [sb(f"prob{i}", [P, S]) for i in range(NT)]
    probT = [sb(f"probT{i}", [P, S]) for i in range(NT)]
    x1 = sb("x1", [P, B * NT, D])
    x1b = sb("x1b", [P, B * NT, D])
    ctxT = sb("ctxT", [P, B, HG, TC])
    k_split = [sb(f"k_split{b}", [QR + MR, NG, TC]) for b in range(B)]
    k_diag = [sb(f"k_diag{b}", [QR + MR, NG, GK]) for b in range(B)]
    v_rows = [sb(f"v_rows{b}", [CR, NC, D]) for b in range(B)]
    v_diag = [sb(f"v_diag{b}", [CR, NC, D]) for b in range(B)]
    ones_diag = sb("ones_diag", [CR, NC, GR])
    q_split = [[sb(f"q_split{b}_{j}", [QR + MR, S]) for j in range(NG)] for b in range(B)]
    max2 = sb("max2", [P, B, NG, NT, HG])
    max2_split = sb("max2_split", [P, B, NG, NT, MR])
    prob2 = [sb(f"prob2_{n}", [CR, S]) for n in range(NG * NC)]
    den_sb = sb("den_sb", [P, S])
    num_sb = sb("num_sb", [P, S])
    den_inv = sb("den_inv", [P, B, NT, NH])
    den_inv8 = sb("den_inv8", [P, NT, NH, HD])
    yT = sb("yT", [P, S])
    x2 = sb("x2", [P, B * NT, D])
    res = sb("res", [P, B * NT, D])
    tT = sb("tT", [P, S])
    tT_hi = [sb(f"tT_hi{b}", [P, S]) for b in range(B)]
    tT_lo = [sb(f"tT_lo{b}", [P, S]) for b in range(B)]
    routT = sb("routT", [P, S])
    logits = sb("logits", [P, B, NT, NE])
    top8 = sb("top8", [P, B, NT, 8])
    top8_at = sb("top8_at", [P, B, NT, 8], u32)
    top_at = sb("top_at", [P, B, NT, TOPK])
    gap = sb("gap", [P, B, NT])
    gap_tanh = sb("gap_tanh", [P, B, NT])
    w_top = sb("w_top", [P, B, TOPK, NT])
    w_hot = sb("w_hot", [P, B, TOPK, NT, NE])
    w_part = sb("w_part", [P, B, TOPK, NT, NE])
    w_all = sb("w_all", [P, B, NT, NE])
    wT = sb("wT", [NE, S])
    wT_split = sb("wT_split", [32 + NE, S])
    pick_f = sb("pick_f", [32 + NE, NE, P])
    pick = sb("pick", [32 + NE, NE, P])
    hid, hidw = prob, probT
    y_sb = sb("y_sb", [P, S])
    out_sb = sb("out_sb", [P, B * NT, D])

    bank = [nc.alloc_psum_tensor(f"bank{n}", [P, 512], f32) for n in range(8)]

    d_x = [sem(f"d_x{b}") for b in range(B)]
    d_const, d_self, d_ctx, d_cross, d_bk, d_ffn, d_eb2, d_ew1, d_ew2, d_out = (
        sem(n) for n in ("d_const", "d_self", "d_ctx", "d_cross", "d_bk", "d_ffn", "d_eb2", "d_ew1",
                         "d_ew2", "d_out"))
    names = ("dve_step pool_step mask_ready aw_mm aw_ready ln_ready "
             "xT_mm xT_ready g_mm g_ready v_mm v_ready s_mm s_max p_ready pT_mm pT_ready o_mm x1_ready "
             "ctxT_mm ctxT_ready k_mm k_hi k_lo k_ready v2_mm v2_rows v2_ready ones_ready "
             "q_mm q_hi q_lo s2_mm s2_max m_split m_mm m_ready st_mm p2_ready pv_mm "
             "den_ready num_ready dT_mm dinv_ready rT_mm yT_ready wp_mm x1b_ready x2_ready "
             "res_ready tT_full tT_hi_ready tT_lo_ready hid_mm rout_ready lg_mm gap_ready tanh_ready "
             "w_ready wT_mm wT_full wT_hi wT_lo pick_ready w1s_ready wb_mm z_mm silu_ready hidw_ready "
             "e_mm y_ready yo_mm out_ready").split()
    q = {n: sem(n) for n in names}
    (dve_step, pool_step, mask_ready, aw_mm, aw_ready, ln_ready,
     xT_mm, xT_ready, g_mm, g_ready, v_mm, v_ready, s_mm, s_max, p_ready, pT_mm, pT_ready, o_mm, x1_ready,
     ctxT_mm, ctxT_ready, k_mm, k_hi, k_lo, k_ready, v2_mm, v2_rows, v2_ready, ones_ready,
     q_mm, q_hi, q_lo, s2_mm, s2_max, m_split, m_mm, m_ready, st_mm, p2_ready, pv_mm,
     den_ready, num_ready, dT_mm, dinv_ready, rT_mm, yT_ready, wp_mm, x1b_ready, x2_ready,
     res_ready, tT_full, tT_hi_ready, tT_lo_ready, hid_mm, rout_ready, lg_mm, gap_ready, tanh_ready,
     w_ready, wT_mm, wT_full, wT_hi, wT_lo, pick_ready, w1s_ready, wb_mm, z_mm, silu_ready, hidw_ready,
     e_mm, y_ready, yo_mm, out_ready) = (q[n] for n in names)

    LN_SEQ = [(0, 0), (0, 1), (1, 0), (1, 1), (2, 0), (2, 1)]

    def ln_count(stage, b):
        return LN_SEQ.index((stage, b)) + 1

    x_rows = x.rearrange("b (t p) d -> p (b t) d", p=P)
    out_rows = out.rearrange("b (t p) d -> p (b t) d", p=P)

    def rows(b):
        return slice(b * NT, (b + 1) * NT)

    with nc.Block() as block:

        @block.sync
        def _(sp):
            sp.dma_start(x_sb[:, rows(0), :], x_rows[:, rows(0), :]).then_inc(d_x[0], 16)
            sp.dma_start(cst[:, :], consts).then_inc(d_const, 16)
            sp.dma_start(x_sb[:, rows(1), :], x_rows[:, rows(1), :]).then_inc(d_x[1], 16)
            sp.dma_start(w1_sb[:, :, :], ew1.rearrange("e d h -> d e h")).then_inc(d_ew1, 16)
            sp.dma_start(ffnw[:, :], ffn_w).then_inc(d_ffn, 16)
            sp.dma_start(eb2_sb[:, :], eb2).then_inc(d_eb2, 16)
            for b in range(B):
                sp.wait_ge(out_ready, b + 1)
                sp.dma_start(out_rows[:, rows(b), :], out_sb[:, rows(b), :]).then_inc(d_out, 16)
            sp.wait_ge(d_out, 16 * B)

        @block.gpsimd
        def _(pool):
            steps = [0]

            def link(ins):
                steps[0] += 1
                ins.then_inc(pool_step, 1)
                pool.wait_ge(pool_step, steps[0])

            g = nc.gpsimd
            for b in range(B):
                link(g.memset(k_split[b][QR:QR + MR, :, :], 1.0))
            link(g.memset(wT_split[:, :], 0.0))
            link(g.memset(pick_f[:, :, :], 0.0))
            pool.wait_ge(d_const, 16)
            g.tensor_copy(ident_b[:, :], ident).then_inc(mask_ready, 1)
            g.tensor_copy(causal_b[:, :], cst[:, C_CAUSAL:C_CAUSAL + P]).then_inc(mask_ready, 1)
            for base in (0, -32):
                link(g.affine_select(out=pick_f[:, :, :], in_=pick_f[:, :, :], compare_op=ALU.not_equal,
                                     fill=1.0, base=base, pattern=[[-1, NE], [0, P]], channel_multiplier=1))
            g.tensor_copy(r(pick[:, :, :]), pick_f[:, :, :]).then_inc(pick_ready, 1)
            vmask = cst[0:CR, C_VMASK:C_VMASK + NC * HG]
            g.tensor_copy(ones_diag[:, :, :].rearrange("p c (h d) -> p (c h) d", d=HD),
                          vmask.unsqueeze(2).broadcast_to([CR, NC * HG, HD])).then_inc(ones_ready, 1)
            hmask = cst[0:QR + MR, C_HMASK:C_HMASK + HG]
            for b in range(B):
                pool.wait_ge(k_lo, b + 1)
                for j in range(NG):
                    g.tensor_tensor(
                        r(k_diag[b][:, j, :]).rearrange("p (h t) -> p h t", h=HG),
                        k_split[b][:, j, :].unsqueeze(1).broadcast_to([QR + MR, HG, TC]),
                        hmask.unsqueeze(2).broadcast_to([QR + MR, HG, TC]), ALU.mult).then_inc(k_ready, 1)
                for c in range(NC):
                    k = CROWS[c]
                    pool.wait_ge(v2_rows, NC * b + c + 1)
                    g.tensor_tensor(
                        v_diag[b][0:k, c, :].rearrange("p (j h d) -> p j h d", j=NG, h=HG),
                        v_rows[b][0:k, c, :].rearrange("p (j h d) -> p j h d", j=NG, h=HG),
                        vmask[0:k, c * HG:(c + 1) * HG].unsqueeze(1).unsqueeze(3)
                        .broadcast_to([k, NG, HG, HD]), ALU.mult).then_inc(v2_ready, 1)
            pool.wait_ge(d_ew1, 16)
            for e in range(NE):
                link(g.tensor_copy(r(w1_hi[:, e, :]), w1_sb[:, e, :]))
                g.tensor_tensor(r(w1_lo[:, e, :]), w1_sb[:, e, :], w1_hi[:, e, :],
                                ALU.subtract).then_inc(w1s_ready, 1)
            for b in range(B):
                pool.wait_ge(x1_ready, NT * (b + 1))
                g.tensor_tensor(x1b[:, rows(b), :], x1[:, rows(b), :],
                                crossw[:, X_BP:X_BP + D].unsqueeze(1).broadcast_to([P, NT, D]),
                                ALU.add).then_inc(x1b_ready, 1)
            for b in range(B):
                pool.wait_ge(ln_ready, NT * ln_count(2, b))
                g.tensor_tensor(res[:, rows(b), :], x2[:, rows(b), :], xn[:, 2, :, :],
                                ALU.add).then_inc(res_ready, 1)

        @block.scalar
        def _(act):
            a = nc.scalar
            act.dma_start(selfw[:, :], self_w).then_inc(d_self, 16)
            act.dma_start(ctx_sb[:, :, :], ctx.rearrange("b t d -> t b d")).then_inc(d_ctx, 16)
            act.dma_start(crossw[:, :], cross_w).then_inc(d_cross, 16)
            act.dma_start(bkrow[:, :], bk_row).then_inc(d_bk, 16)
            act.dma_start(w2_sb[:, :, :, :], ew2.rearrange("e (c h) d -> h e c d", h=P)).then_inc(d_ew2, 16)
            act.wait_ge(aw_mm, 1)
            a.activation(a_sb[:, :], bank[1][:, 0:P], ACT.Copy, scale=float(KD) ** -0.5).then_inc(aw_ready, 1)
            a.activation(w12[:, :], bank[1][:, P:2 * P], ACT.Copy).then_inc(aw_ready, 1)

            def evac_xT(stage, b, dst):
                act.wait_ge(xT_mm, ln_count(stage, b))
                a.activation(dst, bank[0][:, :], ACT.Copy).then_inc(xT_ready, 1)

            def ctx_evac():
                act.wait_ge(ctxT_mm, 1)
                for b in range(B):
                    a.activation(ctxT[:, b, :, :], bank[7][:, b * TC:(b + 1) * TC].unsqueeze(1)
                                 .broadcast_to([P, HG, TC]), ACT.Copy).then_inc(ctxT_ready, 1)

            def k_evac(b):
                act.wait_ge(k_mm, b + 1)
                a.activation(r(k_split[b][0:QR, :, :]),
                             bank[7][0:QR, 0:GK].rearrange("p (j t) -> p j t", j=NG),
                             ACT.Copy).then_inc(k_hi, 1)

            def exp1(b, i):
                act.wait_ge(s_max, NT * b + i + 1)
                if b > 0:
                    act.wait_ge(pT_mm, NT * (b - 1) + i + 1)
                a.activation(prob[i][:, 0:(i + 1) * P], bank[2 + i % 2][:, 0:(i + 1) * P], ACT.Exp,
                             bias=negmax[:, b, i:i + 1], accum_out=rowsum[:, b, i:i + 1]).then_inc(p_ready, 1)

            def pT_evac(b, i):
                act.wait_ge(pT_mm, NT * b + i + 1)
                if b > 0:
                    act.wait_ge(o_mm, NT * (b - 1) + i + 1)
                a.activation(probT[i][:, 0:(i + 1) * P], bank[4 + i % 2][:, 0:(i + 1) * P],
                             ACT.Copy).then_inc(pT_ready, 1)

            for b in range(B):
                evac_xT(0, b, xT[b][:, :])
                act.wait_ge(g_mm, b + 1)
                a.activation(gT[b][:, :], bank[0][:, :], ACT.Copy).then_inc(g_ready, 1)
                if b == 0:
                    ctx_evac()
                exp1(b, 0)
                exp1(b, 1)
                pT_evac(b, 0)
                k_evac(b)
                exp1(b, 2)
                pT_evac(b, 1)
                exp1(b, 3)
                pT_evac(b, 2)
                pT_evac(b, 3)

            def q_evac(b, j):
                act.wait_ge(q_mm, NG * b + j + 1)
                a.activation(r(q_split[b][j][0:QR, :]), bank[4 + j % 2][0:QR, :], ACT.Identity,
                             bias=crossw[0:QR, X_BQ + j:X_BQ + j + 1]).then_inc(q_hi, 1)

            def m_evac(b, j):
                act.wait_ge(m_mm, NG * b + j + 1)
                a.activation(r(q_split[b][j][QR:QR + MR, :]), bank[6][0:MR, :], ACT.Copy).then_inc(m_ready, 1)

            def exp2(b, j, c):
                n = j * NC + c
                act.wait_ge(st_mm, NG * NC * b + n + 1)
                if b > 0:
                    act.wait_ge(pv_mm, b)
                a.activation(prob2[n][0:CROWS[c], :], bank[n % 2][0:CROWS[c], :], ACT.Exp,
                             scale=float(HD) ** -0.5).then_inc(p2_ready, 1)

            for b in range(B):
                evac_xT(1, b, xT[b][:, :])
                q_evac(b, 0)
                q_evac(b, 1)
                for j in range(NG):
                    if j + 2 < NG:
                        q_evac(b, j + 2)
                    m_evac(b, j)
                    for c in range(NC):
                        exp2(b, j, c)
                act.wait_ge(pv_mm, b + 1)
                if b > 0:
                    act.wait_ge(yT_ready, b)
                a.activation(den_sb[:, :], bank[7][:, :], ACT.Copy).then_inc(den_ready, 1)
                a.activation(num_sb[:, :], bank[6][:, :], ACT.Copy).then_inc(num_ready, 1)

            for b in range(B):
                if b > 0:
                    act.wait_ge(hid_mm, b)
                evac_xT(2, b, tT[:, :])
                a.activation(r(tT_hi[b][:, :]), bank[0][:, :], ACT.Copy).then_inc(tT_hi_ready, 1)
                act.wait_ge(hid_mm, b + 1)
                if b > 0:
                    act.wait_ge(lg_mm, b)
                else:
                    act.wait_ge(d_ffn, 16)
                a.activation(routT[:, :], bank[1][:, :], ACT.Silu,
                             bias=ffnw[:, F_RB1:F_RB1 + 1]).then_inc(rout_ready, 1)
                act.wait_ge(gap_ready, b + 1)
                a.activation(gap_tanh[:, b, :], gap[:, b, :], ACT.Tanh, scale=0.5).then_inc(tanh_ready, 1)
                act.wait_ge(wT_mm, b + 1)
                if b > 0:
                    act.wait_ge(e_mm, NU * b)
                a.activation(wT[:, :], bank[1][0:NE, :], ACT.Copy).then_inc(wT_full, 1)
                for u in range(NU):
                    n = NU * b + u
                    act.wait_ge(z_mm, n + 1)
                    if n >= NS:
                        act.wait_ge(hidw_ready, n - NS + 1)
                    a.activation(hid[n % NS][:, :], bank[2 + n % NZ][:, :], ACT.Silu,
                                 bias=ffnw[:, F_EB1 + u:F_EB1 + u + 1]).then_inc(silu_ready, 1)
                act.wait_ge(e_mm, NU * (b + 1))
                if b > 0:
                    act.wait_ge(yo_mm, b)
                a.activation(y_sb[:, :], bank[7][:, :], ACT.Copy).then_inc(y_ready, 1)

        @block.vector
        def _(dve):
            v = nc.vector
            steps = [0]

            def link(ins):
                steps[0] += 1
                ins.then_inc(dve_step, 1)
                dve.wait_ge(dve_step, steps[0])

            def layer_norm(stage, b, src):
                st, mv = stats[:, stage, b], meanvar[:, stage, b]
                for t in range(NT):
                    last = v.bn_stats(st[:, t, :], src[:, b * NT + t, :])
                link(last)
                for t in range(NT):
                    last = v.bn_aggr(mv[:, t, :], st[:, t, :])
                link(last)
                var = rs_v[:, stage, b, :]
                link(v.tensor_scalar(var, mv[:, :, 1], EPS, None, ALU.add))
                link(v.tensor_scalar(rs_i[:, stage, b, :], var.bitcast(i32), 1, None, ALU.arith_shift_right))
                guess = rs_y[:, stage, b]
                link(v.tensor_scalar(guess[:, 0, :], rs_i[:, stage, b, :], -1.0, float(0x5f3759df),
                                     ALU.mult, ALU.add))
                for k in range(3):
                    y0, y1 = guess[:, k, :].bitcast(f32), guess[:, k + 1, :].bitcast(f32)
                    h0, h1 = rs_t[:, stage, b, 2 * k, :], rs_t[:, stage, b, 2 * k + 1, :]
                    link(v.scalar_tensor_tensor(h0, y0, -0.5, y0, ALU.mult, ALU.mult))
                    link(v.tensor_tensor(h1, h0, var, ALU.mult))
                    link(v.scalar_tensor_tensor(y1, h1, 1.5, y0, ALU.add, ALU.mult))
                if b > 0:
                    dve.wait_ge(xT_mm, ln_count(stage, b - 1))
                    if stage == 2:
                        dve.wait_ge(res_ready, b)
                for t in range(NT):
                    v.tensor_scalar(xn[:, stage, t, :], src[:, b * NT + t, :], mv[:, t, 0:1],
                                    guess[:, 3, t:t + 1].bitcast(f32), ALU.subtract,
                                    ALU.mult).then_inc(ln_ready, 1)

            def values(b):
                dve.wait_ge(v_mm, b + 1)
                v.tensor_copy(val[b][:, :, :], bank[1][:, :].rearrange("p (t d) -> p t d", d=D)).then_inc(v_ready, 1)

            def rowmax(b, i):
                dve.wait_ge(s_mm, NT * b + i + 1)
                v.tensor_reduce(negmax[:, b, i:i + 1], bank[2 + i % 2][:, 0:(i + 1) * P], AX.X, ALU.max,
                                negate=True).then_inc(s_max, 1)

            def residual1(b, i):
                dve.wait_ge(p_ready, NT * b + i + 1)
                link(v.reciprocal(rowinv[:, b, i:i + 1], rowsum[:, b, i:i + 1]))
                dve.wait_ge(o_mm, NT * b + i + 1)
                v.scalar_tensor_tensor(x1[:, b * NT + i, :], bank[6 if i % 2 == 0 else 1][:, 0:D],
                                       rowinv[:, b, i:i + 1], x_sb[:, b * NT + i, :], ALU.mult,
                                       ALU.add).then_inc(x1_ready, 1)

            def kv_split(b):
                dve.wait_ge(k_hi, b + 1)
                v.tensor_tensor(r(k_split[b][2 * GR:QR, :, :]),
                                bank[7][2 * GR:QR, 0:GK].rearrange("p (j t) -> p j t", j=NG),
                                k_split[b][2 * GR:QR, :, :], ALU.subtract).then_inc(k_lo, 1)
                dve.wait_ge(v2_mm, b + 1)
                for c in range(NC):
                    k = CROWS[c]
                    v.tensor_tensor(v_rows[b][0:k, c, :], bank[7][0:k, c * D:(c + 1) * D],
                                    crossw[0:k, X_BV:X_BV + D], ALU.add).then_inc(v2_rows, 1)

            dve.wait_ge(d_x[0], 16)
            layer_norm(0, 0, x_sb)
            dve.wait_ge(d_x[1], 16)
            layer_norm(0, 1, x_sb)
            for b in range(B):
                values(b)
                rowmax(b, 0)
                rowmax(b, 1)
                if b == 0:
                    dve.wait_ge(d_cross, 16)
                kv_split(b)
                rowmax(b, 2)
                residual1(b, 0)
                rowmax(b, 3)
                residual1(b, 1)
                residual1(b, 2)
                residual1(b, 3)
                dve.wait_ge(x1_ready, NT * (b + 1))
                layer_norm(1, b, x1)

            def q_rest(b, j):
                dve.wait_ge(q_hi, NG * b + j + 1)
                v.scalar_tensor_tensor(r(q_split[b][j][GR:2 * GR, :]), bank[4 + j % 2][GR:2 * GR, :],
                                       crossw[GR:2 * GR, X_BQ + j:X_BQ + j + 1],
                                       q_split[b][j][GR:2 * GR, :], ALU.add, ALU.subtract).then_inc(q_lo, 1)

            def key_max(b, j):
                for i in range(NT):
                    n = NG * NT * b + NT * j + i
                    dve.wait_ge(s2_mm, n + 1)
                    v.tensor_reduce(max2[:, b, j, i, :],
                                    bank[2 + n % 2][:, 0:GK].rearrange("p (h t) -> p h t", h=HG), AX.X,
                                    ALU.max, negate=True).then_inc(s2_max, 1)
                dve.wait_ge(s2_max, NT * (NG * b + j + 1))
                hi, lo = max2_split[:, b, j, :, 0:HG], max2_split[:, b, j, :, HG:MR]
                link(v.tensor_copy(r(hi), max2[:, b, j, :, :]))
                v.tensor_tensor(r(lo), max2[:, b, j, :, :], hi, ALU.subtract).then_inc(m_split, 1)

            for b in range(B):
                q_rest(b, 0)
                q_rest(b, 1)
                for j in range(NG):
                    key_max(b, j)
                    if j + 2 < NG:
                        q_rest(b, j + 2)
                dve.wait_ge(dT_mm, b + 1)
                link(v.reciprocal(den_inv[:, b, :, :],
                                  bank[7][:, :].rearrange("p (t h d) -> p t h d", t=NT, d=HD)[:, :, :, 0]))
                if b > 0:
                    dve.wait_ge(rT_mm, b)
                v.tensor_copy(den_inv8[:, :, :, :],
                              den_inv[:, b, :, :].unsqueeze(3).broadcast_to([P, NT, NH, HD])
                              ).then_inc(dinv_ready, 1)
                dve.wait_ge(rT_mm, b + 1)
                dve.wait_ge(num_ready, b + 1)
                if b > 0:
                    dve.wait_ge(wp_mm, b)
                v.tensor_tensor(yT[:, :], num_sb[:, :], bank[7][:, :], ALU.mult).then_inc(yT_ready, 1)
                dve.wait_ge(wp_mm, b + 1)
                dve.wait_ge(x1b_ready, b + 1)
                v.tensor_tensor(x2[:, rows(b), :], x1b[:, rows(b), :],
                                bank[6][:, :].rearrange("p (t d) -> p t d", d=D), ALU.add).then_inc(x2_ready, 1)
                dve.wait_ge(x2_ready, b + 1)
                if b > 0:
                    pass
                layer_norm(2, b, x2)

            for b in range(B):
                dve.wait_ge(tT_hi_ready, b + 1)
                v.tensor_tensor(r(tT_lo[b][:, :]), bank[0][:, :], tT_hi[b][:, :], ALU.subtract).then_inc(tT_lo_ready, 1)
                dve.wait_ge(lg_mm, b + 1)
                lg = logits[:, b]
                link(v.tensor_tensor(lg, bank[1][:, 0:NT * NE].rearrange("p (t e) -> p t e", e=NE),
                                     ffnw[:, F_RB2:F_RB2 + NE].unsqueeze(1).broadcast_to([P, NT, NE]), ALU.add))
                for t in range(NT):
                    last = v.max(top8[:, b, t, :], lg[:, t, :])
                link(last)
                v.tensor_tensor(gap[:, b, :], top8[:, b, :, 1], top8[:, b, :, 0], ALU.subtract).then_inc(gap_ready, 1)
                for t in range(NT):
                    last = v.max_index(top8_at[:, b, t, :], top8[:, b, t, :], lg[:, t, :])
                link(last)
                v.tensor_copy(top_at[:, b, :, :], top8_at[:, b, :, 0:TOPK]).then_inc(dve_step, 1)
                steps[0] += 1
                dve.wait_ge(tanh_ready, b + 1)
                v.tensor_scalar(w_top[:, b, 0, :], gap_tanh[:, b, :], -0.5, 0.5, ALU.mult, ALU.add).then_inc(dve_step, 1)
                steps[0] += 1
                link(v.tensor_scalar(w_top[:, b, 1, :], gap_tanh[:, b, :], 0.5, 0.5, ALU.mult, ALU.add))
                for k in range(TOPK):
                    link(v.tensor_tensor(w_hot[:, b, k], cst[:, C_IOTA:C_IOTA + NE].unsqueeze(1)
                                         .broadcast_to([P, NT, NE]),
                                         top_at[:, b, :, k].unsqueeze(2).broadcast_to([P, NT, NE]), ALU.is_equal))
                for k in range(TOPK):
                    link(v.tensor_tensor(w_part[:, b, k], w_hot[:, b, k],
                                         w_top[:, b, k, :].unsqueeze(2).broadcast_to([P, NT, NE]), ALU.mult))
                v.tensor_tensor(w_all[:, b], w_part[:, b, 0], w_part[:, b, 1], ALU.add).then_inc(w_ready, 1)
                dve.wait_ge(wT_full, b + 1)
                if b > 0:
                    dve.wait_ge(wb_mm, NE * b)
                v.tensor_copy(r(wT_split[0:NE, :]), bank[1][0:NE, :]).then_inc(wT_hi, 1)
                dve.wait_ge(wT_hi, b + 1)
                v.tensor_tensor(r(wT_split[32:32 + NE, :]), bank[1][0:NE, :], wT_split[0:NE, :],
                                ALU.subtract).then_inc(wT_lo, 1)
                for u in range(NU):
                    n, e = NU * b + u, NE * b + u // FC
                    dve.wait_ge(silu_ready, n + 1)
                    dve.wait_ge(wb_mm, e + 1)
                    if n >= NS:
                        dve.wait_ge(e_mm, n - NS + 1)
                    v.tensor_tensor(hidw[n % NS][:, :], hid[n % NS][:, :], bank[5 + e % 2][:, :],
                                    ALU.mult).then_inc(hidw_ready, 1)
                dve.wait_ge(yo_mm, b + 1)
                dve.wait_ge(res_ready, b + 1)
                v.tensor_tensor(out_sb[:, rows(b), :], res[:, rows(b), :],
                                bank[0][:, :].rearrange("p (t d) -> p t d", d=D), ALU.add).then_inc(out_ready, 1)

        @block.tensor
        def _(pe):
            mm, tr = nc.tensor.matmul, nc.tensor.transpose

            def cols(i):
                return slice(i * P, (i + 1) * P)

            pe.wait_ge(d_self, 16)
            mm(bank[1][:, 0:P], selfw[:, 0:P], selfw[:, P:2 * P], start=True, stop=True)
            mm(bank[1][:, P:2 * P], selfw[:, 2 * P:3 * P], selfw[:, 3 * P:4 * P], start=True,
               stop=True).then_inc(aw_mm, 1)
            pe.wait_ge(d_const, 16)

            def transposes(stage, b):
                for t in range(NT):
                    pe.wait_ge(ln_ready, NT * (ln_count(stage, b) - 1) + t + 1)
                    last = tr(bank[0][:, cols(t)], xn[:, stage, t, :], ident)
                last.then_inc(xT_mm, 1)

            def scores1(b, i):
                if i >= 2 or b > 0:
                    pe.wait_ge(p_ready, NT * b + i - 1)
                sc = bank[2 + i % 2]
                mm(sc[:, 0:(i + 1) * P], gT[b][:, cols(i)], xT[b][:, 0:(i + 1) * P], start=True, stop=False)
                mm(sc[:, cols(i)], ident_b[:, :], causal_b[:, :], start=False, stop=True).then_inc(s_mm, 1)

            def probs_T(b, i):
                pe.wait_ge(p_ready, NT * b + i + 1)
                if i >= 2 or b > 0:
                    pe.wait_ge(pT_ready, NT * b + i - 1)
                for k in range(i + 1):
                    last = tr(bank[4 + i % 2][:, cols(k)], prob[i][:, cols(k)], ident)
                last.then_inc(pT_mm, 1)

            def attend1(b, i):
                pe.wait_ge(pT_ready, NT * b + i + 1)
                if i >= 2 or (b > 0 and i == 0):
                    pe.wait_ge(x1_ready, NT * b + i - 1)
                if i == 1:
                    pe.wait_ge(v_ready, b + 1)
                for k in range(i + 1):
                    last = mm(bank[6 if i % 2 == 0 else 1][:, 0:D], probT[i][:, cols(k)], val[b][:, k, :],
                              start=(k == 0), stop=(k == i))
                last.then_inc(o_mm, 1)

            def context_T():
                pe.wait_ge(d_ctx, 16)
                for b in range(B):
                    last = tr(bank[7][:, b * TC:(b + 1) * TC], ctx_sb[:, b, :], ident[0:TC, 0:TC])
                last.then_inc(ctxT_mm, 1)

            def keys(b):
                if b == 0:
                    pe.wait_ge(d_cross, 16)
                    pe.wait_ge(d_bk, 16)
                    pe.wait_ge(ctxT_ready, B)
                else:
                    pe.wait_ge(v2_rows, NC * b)
                for j in range(NG):
                    k_out = bank[7][0:QR, j * TC:(j + 1) * TC]
                    mm(k_out, crossw[:, X_WK + j * QR:X_WK + (j + 1) * QR], ctxT[:, b, 0, :], start=True,
                       stop=False)
                    last = mm(k_out, bkrow[0:1, j * QR:(j + 1) * QR], bkrow[0:1, NG * QR:NG * QR + TC],
                              start=False, stop=True)
                last.then_inc(k_mm, 1)

            def context_values(b):
                pe.wait_ge(k_lo, b + 1)
                flat = ctxT[:, b, :, :].rearrange("p h t -> p (h t)")
                for c in range(NC):
                    last = mm(bank[7][0:CROWS[c], cols(c)], flat[:, c * CR:c * CR + CROWS[c]],
                              crossw[:, X_WV:X_WV + D], start=True, stop=True)
                last.then_inc(v2_mm, 1)

            for b in range(B):
                if b > 0:
                    pe.wait_ge(g_ready, b)
                transposes(0, b)
                pe.wait_ge(xT_ready, b + 1)
                pe.wait_ge(aw_ready, 2)
                mm(bank[0][:, :], a_sb[:, :], xT[b][:, :], start=True, stop=True).then_inc(g_mm, 1)
                if b > 0:
                    pe.wait_ge(x1_ready, NT * b)
                for t in range(NT):
                    last = mm(bank[1][:, cols(t)], xT[b][:, cols(t)], w12[:, :], start=True, stop=True)
                last.then_inc(v_mm, 1)
                if b == 0:
                    context_T()
                pe.wait_ge(g_ready, b + 1)
                pe.wait_ge(mask_ready, 2)
                scores1(b, 0)
                scores1(b, 1)
                keys(b)
                probs_T(b, 0)
                scores1(b, 2)
                context_values(b)
                probs_T(b, 1)
                attend1(b, 0)
                scores1(b, 3)
                probs_T(b, 2)
                attend1(b, 1)
                probs_T(b, 3)
                attend1(b, 2)
                attend1(b, 3)

            def queries(b, j):
                if j >= 2 or b > 0:
                    pe.wait_ge(q_lo, NG * b + j - 1)
                elif j == 0:
                    pe.wait_ge(pT_ready, NT * B)
                mm(bank[4 + j % 2][0:QR, :], crossw[:, X_WQ + j * QR:X_WQ + (j + 1) * QR], xT[b][:, :],
                   start=True, stop=True).then_inc(q_mm, 1)

            def scores2(b, j):
                pe.wait_ge(q_lo, NG * b + j + 1)
                pe.wait_ge(k_ready, NG * b + j + 1)
                for i in range(NT):
                    n = NG * NT * b + NT * j + i
                    if n >= 2:
                        pe.wait_ge(s2_max, n - 1)
                    else:
                        pe.wait_ge(p_ready, NT * B)
                    mm(bank[2 + n % 2][:, 0:GK], r(q_split[b][j][0:QR, cols(i)]), r(k_diag[b][0:QR, j, :]),
                       start=True, stop=True).then_inc(s2_mm, 1)

            def maxima_T(b, j):
                pe.wait_ge(m_split, NG * b + j + 1)
                if j > 0:
                    pe.wait_ge(m_ready, NG * b + j)
                elif b > 0:
                    pe.wait_ge(x2_ready, b)
                else:
                    pe.wait_ge(x1_ready, NT * B)
                for i in range(NT):
                    last = tr(bank[6][0:MR, cols(i)], max2_split[:, b, j, i, :], ident)
                last.then_inc(m_mm, 1)

            def scores2_T(b, j):
                pe.wait_ge(m_ready, NG * b + j + 1)
                for c in range(NC):
                    n = j * NC + c
                    if n >= 2 or b > 0:
                        pe.wait_ge(p2_ready, NG * NC * b + n - 1)
                    mm(bank[n % 2][0:CROWS[c], :], r(k_diag[b][:, j, c * CR:c * CR + CROWS[c]]),
                       r(q_split[b][j][:, :]), start=True, stop=True).then_inc(st_mm, 1)

            def attend2(b):
                pe.wait_ge(v2_ready, NC * (b + 1))
                pe.wait_ge(ones_ready, 1)
                pe.wait_ge(p2_ready, NG * NC * (b + 1))
                if b > 0:
                    pe.wait_ge(yT_ready, b)
                for dst, w in ((6, v_diag[b]), (7, None)):
                    for c in range(NC):
                        for j in range(NG):
                            k = CROWS[c]
                            lhsT = ones_diag[0:k, c, :] if w is None else w[0:k, c, j * GR:(j + 1) * GR]
                            last = mm(bank[dst][j * GR:(j + 1) * GR, :], lhsT, prob2[j * NC + c][0:k, :],
                                      start=(c == 0), stop=(c == NC - 1), tile_position=(0, j * GR))
                last.then_inc(pv_mm, 1)

            for b in range(B):
                if b == 0:
                    pe.wait_ge(g_ready, B)
                else:
                    pe.wait_ge(p2_ready, NG * NC * b)
                transposes(1, b)
                pe.wait_ge(xT_ready, ln_count(1, b))
                queries(b, 0)
                queries(b, 1)
                for j in range(NG):
                    scores2(b, j)
                    if j + 2 < NG:
                        queries(b, j + 2)
                    maxima_T(b, j)
                    scores2_T(b, j)
                attend2(b)
                pe.wait_ge(den_ready, b + 1)
                for i in range(NT):
                    last = tr(bank[7][:, cols(i)], den_sb[:, cols(i)], ident)
                last.then_inc(dT_mm, 1)
                pe.wait_ge(dinv_ready, b + 1)
                for i in range(NT):
                    last = tr(bank[7][:, cols(i)],
                              den_inv8[:, i, :, :].rearrange("p h d -> p (h d)"), ident)
                last.then_inc(rT_mm, 1)
                pe.wait_ge(yT_ready, b + 1)
                for i in range(NT):
                    last = mm(bank[6][:, cols(i)], yT[:, cols(i)], crossw[:, X_WP:X_WP + D], start=True,
                              stop=True)
                last.then_inc(wp_mm, 1)

            def hidden(b, u):
                n, e, c = NU * b + u, u // FC, u % FC
                if n >= NZ:
                    pe.wait_ge(silu_ready, n - NZ + 1)
                z = bank[2 + n % NZ][:, :]
                h = slice(c * P, (c + 1) * P)
                pe.wait_ge(w1s_ready, e + 1)
                mm(z, r(w1_hi[:, e, h]), r(tT_hi[b][:, :]), start=True, stop=False)
                mm(z, r(w1_lo[:, e, h]), r(tT_hi[b][:, :]), start=False, stop=False)
                mm(z, r(w1_hi[:, e, h]), r(tT_lo[b][:, :]), start=False, stop=True).then_inc(z_mm, 1)

            def weight_rows(b, e):
                n = NE * b + e
                if n >= 2:
                    pe.wait_ge(hidw_ready, FC * (n - 1))
                mm(bank[5 + n % 2][:, :], r(pick[:, e, :]), r(wT_split[:, :]), start=True,
                   stop=True).then_inc(wb_mm, 1)

            def expert_out(b, u):
                n, e, c = NU * b + u, u // FC, u % FC
                pe.wait_ge(hidw_ready, n + 1)
                mm(bank[7][:, :], w2_sb[:, e, c, :], hidw[n % NS][:, :], start=False,
                   stop=(u == NU - 1)).then_inc(e_mm, 1)

            def finish(b):
                pe.wait_ge(y_ready, b + 1)
                for i in range(NT):
                    last = tr(bank[0][:, cols(i)], y_sb[:, cols(i)], ident)
                last.then_inc(yo_mm, 1)

            for b in range(B):
                if b == 0:
                    pe.wait_ge(p2_ready, NG * NC * B)
                    pe.wait_ge(d_ffn, 16)
                else:
                    pe.wait_ge(out_ready, b)
                transposes(2, b)
                pe.wait_ge(xT_ready, ln_count(2, b))
                if b > 0:
                    pe.wait_ge(wT_lo, b)
                mm(bank[1][:, :], ffnw[:, F_RW1:F_RW1 + P], tT[:, :], start=True, stop=True).then_inc(hid_mm, 1)
                pe.wait_ge(tT_lo_ready, b + 1)
                if b == 0:
                    pe.wait_ge(s2_max, NG * NT * B)
                    pe.wait_ge(q_lo, NG * B)
                hidden(b, 0)
                pe.wait_ge(rout_ready, b + 1)
                for t in range(NT):
                    last = mm(bank[1][:, t * NE:(t + 1) * NE], routT[:, cols(t)], ffnw[:, F_RW2:F_RW2 + NE],
                              start=True, stop=True)
                last.then_inc(lg_mm, 1)
                hidden(b, 1)
                pe.wait_ge(w_ready, b + 1)
                for t in range(NT):
                    last = tr(bank[1][0:NE, cols(t)], w_all[:, b, t, :], ident)
                last.then_inc(wT_mm, 1)
                pe.wait_ge(wT_lo, b + 1)
                if b == 0:
                    pe.wait_ge(pick_ready, 1)
                    pe.wait_ge(d_eb2, 16)
                    pe.wait_ge(x2_ready, B)
                    pe.wait_ge(d_ew2, 16)
                else:
                    pe.wait_ge(y_ready, b)
                mm(bank[7][:, :], eb2_sb[:, :], wT[:, :], start=True, stop=False)
                weight_rows(b, 0)
                for u in range(NU):
                    if u + 2 < NU:
                        hidden(b, u + 2)
                    if u % FC == 0 and u // FC + 1 < NE:
                        weight_rows(b, u // FC + 1)
                    expert_out(b, u)
                finish(b)


def kernel(**inputs):
    import numpy as np
    import concourse.bacc as bacc
    from concourse.bass_utils import run_bass_kernel_spmd

    a = {k: np.ascontiguousarray(v) for k, v in inputs.items()}
    row = np.arange(P)
    causal = np.where(row[None, :] > row[:, None], MASKED, 0.0)
    hrow = np.where(row < QR, (row % GR) // HD, (row - QR) % HG)
    hmask = hrow[:, None] == np.arange(HG)[None, :]
    pair = np.arange(NC)[None, :] * CR + row[:, None]
    vmask = ((pair // TC)[:, :, None] == np.arange(HG)[None, None, :]).reshape(P, NC * HG)
    iota = np.tile(np.arange(NE)[None, :], (P, 1))
    consts = np.concatenate([np.eye(P), causal, hmask, vmask, iota], 1).astype(np.float32)

    def rep(w):
        parts = [w[..., j * GR:(j + 1) * GR] for j in range(NG) for _ in range(REPS)]
        return np.concatenate(parts, -1)

    def across(v):
        return np.tile(v[None, :], (P, 1))

    self_w = np.concatenate([a["L0_attn_w_q"].T, a["L0_attn_w_k"].T, a["L0_attn_w_v1"].T,
                             a["L0_attn_w_v2"]], 1)
    bq = np.concatenate([rep(a["L0_xattn_bq"]).reshape(NG, QR).T, np.zeros((P - QR, NG), np.float32)], 0)
    cross_w = np.concatenate([rep(a["L0_xattn_Wq"].T), rep(a["L0_xattn_Wk"].T), a["L0_xattn_Wv"].T,
                              a["L0_xattn_Wp"].T, bq, across(a["L0_xattn_bv"]), across(a["L0_xattn_bp"])], 1)
    bk_row = np.concatenate([rep(a["L0_xattn_bk"]), np.ones(TC, np.float32)])[None, :]
    ffn_w = np.concatenate([a["L0_ffn_rw1"], a["L0_ffn_rw2"], a["L0_ffn_rb1"][:, None],
                            a["L0_ffn_eb1"].reshape(NU, P).T, across(a["L0_ffn_rb2"])], 1)
    arrays = {"x": a["x"], "ctx": a["ctx_1024"], "consts": consts, "self_w": self_w, "cross_w": cross_w,
              "bk_row": bk_row, "ffn_w": ffn_w, "eb2": a["L0_ffn_eb2"], "ew1": a["L0_ffn_ew1"],
              "ew2": a["L0_ffn_ew2"]}
    arrays = {k: np.ascontiguousarray(v) for k, v in arrays.items()}
    nc = bacc.Bacc("TRN2", target_bir_lowering=False, num_devices=1)
    aps = [nc.dram_tensor(f"in_{k}", v.shape, mybir.dt.float32, kind="ExternalInput").ap()
           for k, v in arrays.items()]
    out = nc.dram_tensor("out", (B, S, D), mybir.dt.float32, kind="ExternalOutput").ap()
    decoder_block(nc, *aps, out)
    result = run_bass_kernel_spmd(nc, [{f"in_{k}": v for k, v in arrays.items()}], core_ids=[0])
    return result.results[0]["out"]
```

```python
import concourse.bass as bass
from concourse import mybir

B, S, D = 2, 512, 128
P = 128
NT = S // P
KD = 64
TC = 77
NH, HD = 16, 8
HG = 4
NG = NH // HG
GR = HG * HD
REPS = 3
QR = REPS * GR
MR = 2 * HG
GK = HG * TC
NC = 3
CR = -(-GK // NC)
CROWS = [min(CR, GK - c * CR) for c in range(NC)]
NE, FH, TOPK = 8, 256, 2
FC = FH // P
NU = NE * FC
EPS = 1e-5
MASKED = -3.0e38
S1_ORDER = """S00 S01 M00 P10 M01 T00 S02 S10 M02 M10 A00 T01 S03 R00 M03 S11 M11 A01 R01 T02 T10 A02 R02 S12
 M12 T03 A10 R10 A03 R03 N00 N01 T11 S13 M13 A11 R11 N02 T12 X01 A12 Q00 R12 T13 Q01 A13 R13 Q02 Q03 L00 N10
 L01 N11 N12 X11"""
GROUP_ORDER = "00 01 02 03 10 11 12 13"
MORE_QUERIES = {1: [(1, 0), (1, 1)], 2: [(1, 2), (1, 3)]}
PARTS2 = dict(a=["attend2:0"], b=["attend2:1"], c=["attend2:2", "den_copy"], d=["attend2:3"], e=["attend2:4"],
              f=["attend2:5", "num_copy"], T=["den_T", "den_inverse"], K=["den_back", "y_scale"],
              P=["project", "residual2"], N=["norm3:0", "norm3:1"], M=["norm3:2"],
              Z=["t_T:2", "t_copy:2", "t_lo"], R=["router", "router_tanh", "router_gate"],
              G=["logits", "top2:0", "tanh"], H=["top2:1"], W=["weights_T", "weights_copy", "weights_split"],
              x=["hidden:0", "silu:0"], y=["hidden:1", "silu:1"], z=["hidden:2", "silu:2"])
TAIL_FILL = {5: "a0 b0 c0 d0 e0 f0 T0", 6: "K0 P0 N0", 7: "M0", 8: "a1 Z0 b1 R0 c1 x0 G0 d1 H0 y0 e1 z0 f1 W0"}
NS = 3

C_ID, C_CAUSAL, C_HMASK, C_VMASK, C_IOTA = 0, 128, 256, 260, 272
C_PICK = 280
C_END = 288
X_WQ, X_WK, X_WV, X_WP = 0, 384, 768, 896
X_BQ, X_BV, X_BP, X_END = 1024, 1028, 1156, 1284
F_RW1, F_RW2, F_RB1, F_EB1, F_RB2, F_END = 0, 128, 136, 137, 153, 161


def schedule():
    out = []

    def add(b, *steps):
        for step in steps:
            name, _, i = step.partition(":")
            out.append((name, b, int(i or 0)))

    def tile1(k, b, n, what):
        steps = {"S": ("scores1",), "M": ("rowmax1", "exp1"), "T": ("probs_T", "probs_copy"),
                 "A": ("attend1",), "R": ("rowinv", "residual1", "stats1")}[what]
        add(b, *(f"{s}:{n}" for s in steps))

    units = [(int(u[0]), int(u[1])) for u in GROUP_ORDER.split()]

    def unit(k, name, i=0, per=1):
        if 0 <= k < len(units):
            b, j = units[k]
            out.append((name, b, per * j + i))

    def queries(b, j):
        add(b, f"query:{j}", f"query_hi:{j}", f"query_lo:{j}")

    def slot(k, *more):
        def scores(i):
            unit(k + 1, "scores2", i, NT)
            unit(k + 1, "rowmax2", i, NT)

        def probs(c):
            unit(k - 1, "keyscores2", c, NC)
            unit(k - 1, "exp2", c, NC)

        probs(0)
        scores(0)
        probs(1)
        scores(1)
        unit(k, "maxima_T")
        unit(k, "maxima_row")
        for b, j in more:
            add(b, f"query:{j}")
        scores(2)
        probs(2)
        scores(3)
        unit(k + 1, "max_split")
        for b, j in more:
            add(b, f"query_hi:{j}", f"query_lo:{j}")

    add(0, "norm1:0", "norm1:1", "context_T", "context_copy", "keys", "keys_hi", "values")
    add(1, "norm1:1")
    add(0, "x_T:0", "x_copy:0", "keys_lo", "value_rows")
    add(1, "keys", "keys_hi", "keys_lo")
    add(0, "project1", "g_copy", "val_copy")
    for what in S1_ORDER.split():
        kind, b, n = what[0], int(what[1]), int(what[2])
        if kind == "P":
            add(b, "x_T:0", "x_copy:0", "values", "value_rows", "project1", "g_copy", "val_copy")
        elif kind == "N":
            add(b, f"norm2:{n}")
        elif kind == "X":
            add(b, "x_T:1", "x_copy:1")
        elif kind == "Q":
            queries(b, n)
        elif kind == "L":
            slot(n - 1)
        else:
            tile1(0, b, n, kind)

    for k in range(1, len(units) + 1):
        slot(k, *MORE_QUERIES.get(k, ()))
        for step in TAIL_FILL.get(k, "").split():
            add(int(step[-1]), *PARTS2[step[:-1]])

    def finish2(b):
        yield ["den_T", "den_inverse"]
        yield ["den_back", "y_scale"]
        yield ["project", "residual2"]
        for part in range(3):
            yield [f"norm3:{part}"]
        for part in "Z R x G H y z W".split():
            yield PARTS2[part]

    def experts(b):
        yield ["weight_row:0", "scale:0"]
        for u in range(NU):
            step = []
            if u + 1 < NU:
                if (u + 1) % FC == 0:
                    step.append(f"weight_row:{(u + 1) // FC}")
                step.append(f"scale:{u + 1}")
            if 3 <= u + 2 < NU:
                step += [f"hidden:{u + 2}", f"silu:{u + 2}"]
            step.append(f"expert:{u}")
            yield step
        yield ["y_copy", "finish", "add_rows"]

    first = list(experts(0))
    second = list(finish2(1)) + list(experts(1))
    for n in range(max(len(first), len(second))):
        for b, steps in ((0, first), (1, second)):
            if n < len(steps):
                add(b, *steps[n])
    return out


def uses(steps, kinds):
    count, use = [0] * B, {}
    for step, b, i in steps:
        if step in kinds:
            use[step, b, i] = count[b]
            count[b] += 1
    return use


def decoder_block(nc, x, ctx, consts, self_w, cross_w, bk_row, ffn_w, eb2, ew1, ew2, out):
    f32, f32r, bf16, u32, i32 = (mybir.dt.float32, mybir.dt.float32r, mybir.dt.bfloat16,
                                 mybir.dt.uint32, mybir.dt.int32)
    ALU, ACT, AX = mybir.AluOpType, mybir.ActivationFunctionType, mybir.AxisListType

    def sb(name, shape, dt=f32):
        return nc.alloc_sbuf_tensor(name, shape, dt)

    def sb2(name, shape, dt=f32):
        return [sb(f"{name}{b}", shape, dt) for b in range(B)]

    def sem(name):
        return nc.alloc_semaphore(name)

    def sem2(name):
        return [sem(f"{name}{b}") for b in range(B)]

    def r(ap):
        return ap.bitcast(f32r)

    x_sb = sb2("x_sb", [P, NT, D])
    cst = sb("cst", [P, C_END])
    ident = cst[:, C_ID:C_ID + P]
    ident_b = sb("ident_b", [P, P], bf16)
    causal_b = sb("causal_b", [P, P], bf16)
    selfw = sb("selfw", [KD, 4 * P])
    crossw = sb("crossw", [P, X_END])
    bkrow = sb("bkrow", [1, NG * QR + TC])
    ffnw = sb("ffnw", [P, F_END])
    eb2_sb = sb("eb2_sb", [NE, D])
    ctx_sb = sb("ctx_sb", [TC, B, D])
    w1_sb = sb("w1_sb", [P, NE, FH])
    w2_sb = sb("w2_sb", [P, NE, FC, D])
    w1_hi = sb("w1_hi", [P, NE, FH])
    w1_lo = sb("w1_lo", [P, NE, FH])
    stats = sb("stats", [P, 3, B, NT, 6])
    meanvar = sb("meanvar", [P, 3, B, NT, 2])
    ln_var = sb("ln_var", [P, 3, B, NT])
    ln_half = sb("ln_half", [P, 3, B, NT], i32)
    ln_root = sb("ln_root", [P, 3, 4, B, NT], i32)
    ln_tmp = sb("ln_tmp", [P, 3, 6, B, NT])
    xn = sb2("xn", [P, NT, D])
    a_sb = sb("a_sb", [P, P])
    w12 = sb("w12", [P, P])
    xT = sb2("xT", [P, S])
    gT = sb2("gT", [P, S])
    val = sb2("val", [P, NT, D])
    negmax = sb("negmax", [P, B, NT])
    rowsum = sb("rowsum", [P, B, NT])
    rowinv_sb = sb("rowinv", [P, B, NT])
    prob = [[sb(f"prob{b}_{i}", [P, (i + 1) * P]) for i in range(NT)] for b in range(B)]
    probT = [[sb(f"probT{b}_{i}", [P, (i + 1) * P]) for i in range(NT)] for b in range(B)]
    x1 = sb2("x1", [P, NT, D])
    x1b = sb2("x1b", [P, NT, D])
    ctxT = sb("ctxT", [P, B, HG, TC])
    k_split = sb2("k_split", [QR + MR, NG, TC])
    k_diag = sb2("k_diag", [QR + MR, NG, GK])
    v_rows = sb2("v_rows", [CR, NC, D])
    v_diag = sb2("v_diag", [CR, NC, D])
    ones_diag = sb("ones_diag", [CR, NC, GR])
    q_split = [[sb(f"q_split{b}_{j}", [QR + MR, S]) for j in range(NG)] for b in range(B)]
    max2 = sb("max2", [P, B, NG, NT, HG])
    max2_split = sb("max2_split", [P, B, NG, NT, MR])
    prob2 = [[sb(f"prob2_{b}_{n}", [P, S]) for n in range(NG * NC)] for b in range(B)]
    den_inv = sb("den_inv", [P, B, NT, NH])
    den_sb = [prob[b][NT - 1] for b in range(B)]
    num_sb = [probT[b][NT - 1] for b in range(B)]
    den_inv8, yT = val, gT
    x2 = x1b
    res = x_sb
    tT_hi = sb2("tT_hi", [P, S])
    tT_lo = sb2("tT_lo", [P, S])
    logits = sb("logits", [P, B, NT, NE])
    top8 = sb("top8", [P, B, NT, 8])
    top8_at = sb("top8_at", [P, B, NT, 8], u32)
    top_at = sb("top_at", [P, B, NT, TOPK])
    gap = sb("gap", [P, B, NT])
    gap_tanh = sb("gap_tanh", [P, B, NT])
    w_top = sb("w_top", [P, B, TOPK, NT])
    w_hot = sb("w_hot", [P, B, TOPK, NT, NE])
    w_part = sb("w_part", [P, B, TOPK, NT, NE])
    w_all = sb("w_all", [P, B, NT, NE])
    wT_split = sb2("wT_split", [32 + NE, S])
    pick = sb("pick", [32 + NE, NE])
    tT = [prob2[b][0] for b in range(B)]
    routT = [prob2[b][1] for b in range(B)]
    y_sb = [prob2[b][2] for b in range(B)]
    hid = [prob2[b][3:3 + NS] for b in range(B)]
    hidw = [prob2[b][3 + NS:3 + 2 * NS] for b in range(B)]
    wT = [prob2[b][3 + 2 * NS] for b in range(B)]
    out_sb = x1
    router_z, router_th = y_sb, [prob2[b][4 + 2 * NS] for b in range(B)]

    bank = [[nc.alloc_psum_tensor(f"bank{b}_{n}", [P, 512], f32) for n in range(4)] for b in range(B)]
    T, U, V, W = ([bank[b][n] for b in range(B)] for n in range(4))

    d_const, d_self, d_ctx, d_cross, d_bk, d_ffn, d_eb2, d_ew1, d_ew2, d_out = (
        sem(n) for n in ("d_const", "d_self", "d_ctx", "d_cross", "d_bk", "d_ffn", "d_eb2", "d_ew1",
                         "d_ew2", "d_out"))
    d_x = sem2("d_x")
    dve_step, pool_step, mask_ready, aw_mm, aw_ready, ctxT_mm, ctxT_ready, ones_ready, pick_ready, w1_ready = (
        sem(n) for n in ("dve_step", "pool_step", "mask_ready", "aw_mm", "aw_ready", "ctxT_mm",
                         "ctxT_ready", "ones_ready", "pick_ready", "w1_ready"))
    norm_ready, norm_T_mm, norm_T_ready = (sem2(n) for n in ("norm_ready", "norm_T_mm", "norm_T_ready"))
    g_mm, g_ready, v_mm, v_ready = (sem2(n) for n in ("g_mm", "g_ready", "v_mm", "v_ready"))
    k_mm, k_hi, k_lo, k_ready = (sem2(n) for n in ("k_mm", "k_hi", "k_lo", "k_ready"))
    v2_mm, v2_rows, v2_ready = (sem2(n) for n in ("v2_mm", "v2_rows", "v2_ready"))
    s_mm, s_max, p_ready = (sem2(n) for n in ("s_mm", "s_max", "p_ready"))
    pT_mm, pT_ready, o_mm, x1_ready, x1b_ready = (
        sem2(n) for n in ("pT_mm", "pT_ready", "o_mm", "x1_ready", "x1b_ready"))
    inv_ready, stat_ready, aggr_ready = (sem2(n) for n in ("inv_ready", "stat_ready", "aggr_ready"))
    q_mm, q_hi, vw_read = (sem2(n) for n in ("q_mm", "q_hi", "vw_read"))
    s2_mm, m_split, tu_mm, tu_read = (sem2(n) for n in ("s2_mm", "m_split", "tu_mm", "tu_read"))
    den_mm, num_mm, den_ready, num_ready, dT_mm, dinv_ready, rT_mm, yT_ready, wp_mm, x2_ready = (
        sem2(n) for n in ("den_mm", "num_mm", "den_ready", "num_ready", "dT_mm", "dinv_ready", "rT_mm", "yT_ready",
                          "wp_mm", "x2_ready"))
    res_ready, tT_hi_ready, tT_lo_ready, rout_tanh, rout_z, hid_mm, rout_ready, lg_mm, lg_ready, gap_ready, tanh_ready = (
        sem2(n) for n in ("res_ready", "tT_hi_ready", "tT_lo_ready", "rout_tanh", "rout_z", "hid_mm", "rout_ready", "lg_mm",
                          "lg_ready", "gap_ready", "tanh_ready"))
    w_ready, wT_mm, wT_full, wT_hi, wT_lo = (
        sem2(n) for n in ("w_ready", "wT_mm", "wT_full", "wT_hi", "wT_lo"))
    wb_mm, z_mm, silu_ready, hidw_ready, e_mm, y_ready, yo_mm, out_ready = (
        sem2(n) for n in ("wb_mm", "z_mm", "silu_ready", "hidw_ready", "e_mm", "y_ready", "yo_mm",
                          "out_ready"))

    SCHEDULE = schedule()
    vw_use = uses(SCHEDULE, ("query", "scores2"))
    tu_use = {at: n + 1 for at, n in uses(SCHEDULE, ("maxima_T", "keyscores2")).items()}
    x_rows = x.rearrange("b (t p) d -> p b t d", p=P)
    out_rows = out.rearrange("b (t p) d -> p b t d", p=P)

    with nc.Block() as block:

        @block.sync
        def _(sp):
            sp.dma_start(x_sb[0][:, :, :], x_rows[:, 0]).then_inc(d_x[0], 16)
            sp.dma_start(cst[:, :], consts).then_inc(d_const, 16)
            sp.dma_start(x_sb[1][:, :, :], x_rows[:, 1]).then_inc(d_x[1], 16)
            sp.dma_start(bkrow[:, :], bk_row).then_inc(d_bk, 16)
            sp.dma_start(w1_sb[:, :, :], ew1.rearrange("e d h -> d e h")).then_inc(d_ew1, 16)
            sp.dma_start(ffnw[:, :], ffn_w).then_inc(d_ffn, 16)
            sp.dma_start(eb2_sb[:, :], eb2).then_inc(d_eb2, 16)
            for b in range(B):
                sp.wait_ge(out_ready[b], 1)
                sp.dma_start(out_rows[:, b], out_sb[b][:, :, :]).then_inc(d_out, 16)
            sp.wait_ge(d_out, 16 * B)

        @block.gpsimd
        def _(pool):
            g = nc.gpsimd
            steps = [0]

            def link(ins):
                steps[0] += 1
                ins.then_inc(pool_step, 1)
                pool.wait_ge(pool_step, steps[0])

            for b in range(B):
                link(g.memset(k_split[b][QR:QR + MR, :, :], 1.0))
            for b in range(B):
                link(g.memset(wT_split[b][:, :], 0.0))
            pool.wait_ge(d_const, 16)
            g.tensor_copy(ident_b[:, :], ident).then_inc(mask_ready, 1)
            g.tensor_copy(causal_b[:, :], cst[:, C_CAUSAL:C_CAUSAL + P]).then_inc(mask_ready, 1)
            vmask = cst[0:CR, C_VMASK:C_VMASK + NC * HG]
            g.tensor_copy(ones_diag[:, :, :].rearrange("p c (h d) -> p (c h) d", d=HD),
                          vmask.unsqueeze(2).broadcast_to([CR, NC * HG, HD])).then_inc(ones_ready, 1)
            hmask = cst[0:QR + MR, C_HMASK:C_HMASK + HG]
            for b in range(B):
                pool.wait_ge(k_lo[b], 1)
                for j in range(NG):
                    g.tensor_tensor(
                        r(k_diag[b][:, j, :]).rearrange("p (h t) -> p h t", h=HG),
                        k_split[b][:, j, :].unsqueeze(1).broadcast_to([QR + MR, HG, TC]),
                        hmask.unsqueeze(2).broadcast_to([QR + MR, HG, TC]), ALU.mult).then_inc(k_ready[b], 1)
            for b in range(B):
                for c in range(NC):
                    k = CROWS[c]
                    pool.wait_ge(v2_rows[b], c + 1)
                    g.tensor_tensor(
                        v_diag[b][0:k, c, :].rearrange("p (j h d) -> p j h d", j=NG, h=HG),
                        v_rows[b][0:k, c, :].rearrange("p (j h d) -> p j h d", j=NG, h=HG),
                        vmask[0:k, c * HG:(c + 1) * HG].unsqueeze(1).unsqueeze(3)
                        .broadcast_to([k, NG, HG, HD]), ALU.mult).then_inc(v2_ready[b], 1)
            g.tensor_copy(r(pick[:, :]), cst[0:32 + NE, C_PICK:C_PICK + NE]).then_inc(pick_ready, 1)
            pool.wait_ge(d_ew1, 16)
            for e in range(NE):
                link(g.tensor_copy(r(w1_hi[:, e, :]), w1_sb[:, e, :]))
                g.tensor_tensor(r(w1_lo[:, e, :]), w1_sb[:, e, :], w1_hi[:, e, :],
                                ALU.subtract).then_inc(w1_ready, 1)
                if e % 4 == 3:
                    b = e // 4
                    pool.wait_ge(x1_ready[b], NT)
                    g.tensor_tensor(x1b[b][:, :, :], x1[b][:, :, :],
                                    crossw[:, X_BP:X_BP + D].unsqueeze(1).broadcast_to([P, NT, D]),
                                    ALU.add).then_inc(x1b_ready[b], 1)
            for b in range(B):
                pool.wait_ge(norm_ready[b], 3 * NT)
                g.tensor_tensor(res[b][:, :, :], x2[b][:, :, :], xn[b][:, :, :], ALU.add).then_inc(res_ready[b], 1)

        @block.scalar
        def _(act):
            a = nc.scalar
            act.dma_start(selfw[:, :], self_w).then_inc(d_self, 16)
            act.dma_start(ctx_sb[:, :, :], ctx.rearrange("b t d -> t b d")).then_inc(d_ctx, 16)
            act.dma_start(crossw[:, :], cross_w).then_inc(d_cross, 16)
            act.dma_start(w2_sb[:, :, :, :], ew2.rearrange("e (c h) d -> h e c d", h=P)).then_inc(d_ew2, 16)
            act.wait_ge(aw_mm, 1)
            a.activation(a_sb[:, :], T[1][:, 0:P], ACT.Copy, scale=float(KD) ** -0.5).then_inc(aw_ready, 1)
            a.activation(w12[:, :], T[1][:, P:2 * P], ACT.Copy).then_inc(aw_ready, 1)

            def x_copy(b, stage):
                act.wait_ge(norm_T_mm[b], stage + 1)
                a.activation(xT[b][:, :], T[b][:, :], ACT.Copy).then_inc(norm_T_ready[b], 1)

            def context_copy(b, _):
                act.wait_ge(ctxT_mm, 1)
                for n in range(B):
                    a.activation(ctxT[:, n, :, :], W[0][:, n * TC:(n + 1) * TC].unsqueeze(1)
                                 .broadcast_to([P, HG, TC]), ACT.Copy).then_inc(ctxT_ready, 1)

            def g_copy(b, _):
                act.wait_ge(g_mm[b], 1)
                a.activation(gT[b][:, :], T[b][:, :], ACT.Copy).then_inc(g_ready[b], 1)

            def keys_hi(b, _):
                act.wait_ge(k_mm[b], 1)
                a.activation(r(k_split[b][0:QR, :, :]),
                             W[b][0:QR, 0:GK].rearrange("p (j t) -> p j t", j=NG), ACT.Copy).then_inc(k_hi[b], 1)

            def exp1(b, n):
                i = NT - 1 - n
                act.wait_ge(s_max[b], n + 1)
                a.activation(prob[b][i][:, :], (V, U)[n % 2][b][:, 0:(i + 1) * P], ACT.Exp,
                             bias=negmax[:, b, i:i + 1], accum_out=rowsum[:, b, i:i + 1]).then_inc(p_ready[b], 1)

            def probs_copy(b, n):
                i = NT - 1 - n
                act.wait_ge(pT_mm[b], n + 1)
                a.activation(probT[b][i][:, :], W[b][:, 0:(i + 1) * P], ACT.Copy).then_inc(pT_ready[b], 1)

            def query_hi(b, j):
                act.wait_ge(q_mm[b], j + 1)
                a.activation(r(q_split[b][j][0:QR, :]), (V, W)[vw_use["query", b, j] % 2][b][0:QR, :],
                             ACT.Identity, bias=crossw[0:QR, X_BQ + j:X_BQ + j + 1]).then_inc(q_hi[b], 1)

            def maxima_row(b, j):
                n = tu_use["maxima_T", b, j]
                act.wait_ge(tu_mm[b], n)
                a.activation(r(q_split[b][j][QR:QR + MR, :]), (T, U)[n % 2][b][0:MR, :],
                             ACT.Copy).then_inc(tu_read[b], 1)

            def exp2(b, at):
                n, c = tu_use["keyscores2", b, at], at % NC
                act.wait_ge(tu_mm[b], n)
                a.activation(prob2[b][at][0:CROWS[c], :], (T, U)[n % 2][b][0:CROWS[c], :],
                             ACT.Exp, scale=float(HD) ** -0.5).then_inc(tu_read[b], 1)

            def den_copy(b, _):
                act.wait_ge(den_mm[b], 1)
                a.activation(den_sb[b][:, :], W[b][:, :], ACT.Copy).then_inc(den_ready[b], 1)

            def num_copy(b, _):
                act.wait_ge(num_mm[b], 1)
                a.activation(num_sb[b][:, :], V[b][:, :], ACT.Copy).then_inc(num_ready[b], 1)

            def t_copy(b, stage):
                act.wait_ge(norm_T_mm[b], stage + 1)
                a.activation(tT[b][:, :], T[b][:, :], ACT.Copy).then_inc(norm_T_ready[b], 1)
                a.activation(r(tT_hi[b][:, :]), T[b][:, :], ACT.Copy).then_inc(tT_hi_ready[b], 1)

            def router_tanh(b, _):
                act.wait_ge(d_ffn, 16)
                act.wait_ge(hid_mm[b], 1)
                a.activation(router_z[b][:, :], U[b][:, :], ACT.Identity,
                             bias=ffnw[:, F_RB1:F_RB1 + 1]).then_inc(rout_z[b], 1)
                act.wait_ge(rout_z[b], 1)
                a.activation(router_th[b][:, :], router_z[b][:, :], ACT.Tanh,
                             scale=0.5).then_inc(rout_tanh[b], 1)

            def tanh(b, _):
                act.wait_ge(gap_ready[b], 1)
                a.activation(gap_tanh[:, b, :], gap[:, b, :], ACT.Tanh, scale=0.5).then_inc(tanh_ready[b], 1)

            def weights_copy(b, _):
                act.wait_ge(wT_mm[b], 1)
                a.activation(wT[b][0:NE, :], V[b][0:NE, :], ACT.Copy).then_inc(wT_full[b], 1)

            def silu(b, u):
                act.wait_ge(z_mm[b], u + 1)
                if u >= NS:
                    act.wait_ge(hidw_ready[b], u - NS + 1)
                a.activation(hid[b][u % NS][:, :], (T, U)[u % 2][b][:, :], ACT.Silu,
                             bias=ffnw[:, F_EB1 + u:F_EB1 + u + 1]).then_inc(silu_ready[b], 1)

            def y_copy(b, _):
                act.wait_ge(e_mm[b], NU)
                a.activation(y_sb[b][:, :], W[b][:, :], ACT.Copy).then_inc(y_ready[b], 1)

            parts = dict(x_copy=x_copy, context_copy=context_copy, g_copy=g_copy, keys_hi=keys_hi, exp1=exp1,
                         probs_copy=probs_copy, query_hi=query_hi, maxima_row=maxima_row, exp2=exp2,
                         den_copy=den_copy, num_copy=num_copy, t_copy=t_copy, router_tanh=router_tanh,
                         tanh=tanh, weights_copy=weights_copy, silu=silu, y_copy=y_copy)
            for step, b, i in SCHEDULE:
                if step in parts:
                    parts[step](b, i)

        @block.vector
        def _(dve):
            v = nc.vector
            steps = [0]

            def mark(ins):
                steps[0] += 1
                ins.then_inc(dve_step, 1)

            def link(ins):
                mark(ins)
                dve.wait_ge(dve_step, steps[0])

            def row_stats(stage, b, t, src):
                v.bn_stats(stats[:, stage, b, t, :], src[:, t, :]).then_inc(stat_ready[b], 1)

            def reciprocal_root(stage, b, part):
                var, half, root = ln_var[:, stage, b], ln_half[:, stage, b], ln_root[:, stage, :, b]
                if part == 0:
                    link(v.tensor_scalar(var, meanvar[:, stage, b, :, 1], EPS, None, ALU.add))
                    link(v.tensor_scalar(half, var.bitcast(i32), 1, None, ALU.arith_shift_right))
                    link(v.tensor_scalar(root[:, 0], half, -1.0, float(0x5f3759df), ALU.mult, ALU.add))
                for k in ((0,), (1, 2))[part]:
                    y0, y1 = root[:, k].bitcast(f32), root[:, k + 1].bitcast(f32)
                    h0, h1 = ln_tmp[:, stage, 2 * k, b], ln_tmp[:, stage, 2 * k + 1, b]
                    link(v.scalar_tensor_tensor(h0, y0, -0.5, y0, ALU.mult, ALU.mult))
                    link(v.tensor_tensor(h1, h0, var, ALU.mult))
                    link(v.scalar_tensor_tensor(y1, h1, 1.5, y0, ALU.add, ALU.mult))

            def row_aggregates(stage, b):
                dve.wait_ge(stat_ready[b], NT * (stage + 1))
                for t in range(NT):
                    v.bn_aggr(meanvar[:, stage, b, t, :], stats[:, stage, b, t, :]).then_inc(aggr_ready[b], 1)
                dve.wait_ge(aggr_ready[b], NT * (stage + 1))

            def normalise(stage, b, src):
                if stage > 0:
                    dve.wait_ge(norm_T_mm[b], stage)
                for t in range(NT):
                    v.tensor_scalar(xn[b][:, t, :], src[:, t, :], meanvar[:, stage, b, t, 0:1],
                                    ln_root[:, stage, 3, b, t:t + 1].bitcast(f32), ALU.subtract,
                                    ALU.mult).then_inc(norm_ready[b], 1)

            def norm1(b, part):
                if part == 0:
                    for n in range(B):
                        dve.wait_ge(d_x[n], 16)
                        for t in range(NT):
                            row_stats(0, n, t, x_sb[n])
                    for n in range(B):
                        row_aggregates(0, n)
                    for k in range(2):
                        reciprocal_root(0, slice(0, B), k)
                else:
                    normalise(0, b, x_sb[b])

            def norm2(b, part):
                if part == 0:
                    row_aggregates(1, b)
                if part < 2:
                    reciprocal_root(1, b, part)
                else:
                    normalise(1, b, x1[b])

            def norm3(b, part):
                if part == 0:
                    dve.wait_ge(x2_ready[b], 1)
                    for t in range(NT):
                        row_stats(2, b, t, x2[b])
                    row_aggregates(2, b)
                if part < 2:
                    reciprocal_root(2, b, part)
                else:
                    normalise(2, b, x2[b])

            def val_copy(b, _):
                dve.wait_ge(v_mm[b], 1)
                v.tensor_copy(val[b][:, :, :], U[b][:, :].rearrange("p (t d) -> p t d", d=D)
                              ).then_inc(v_ready[b], 1)

            def keys_lo(b, _):
                dve.wait_ge(k_hi[b], 1)
                v.tensor_tensor(r(k_split[b][2 * GR:QR, :, :]),
                                W[b][2 * GR:QR, 0:GK].rearrange("p (j t) -> p j t", j=NG),
                                k_split[b][2 * GR:QR, :, :], ALU.subtract).then_inc(k_lo[b], 1)

            def value_rows(b, _):
                dve.wait_ge(d_cross, 16)
                dve.wait_ge(v2_mm[b], 1)
                for c in range(NC):
                    k = CROWS[c]
                    v.tensor_tensor(v_rows[b][0:k, c, :], V[b][0:k, c * D:(c + 1) * D],
                                    crossw[0:k, X_BV:X_BV + D], ALU.add).then_inc(v2_rows[b], 1)

            def rowmax1(b, n):
                i = NT - 1 - n
                dve.wait_ge(s_mm[b], n + 1)
                v.tensor_reduce(negmax[:, b, i:i + 1], (V, U)[n % 2][b][:, 0:(i + 1) * P], AX.X, ALU.max,
                                negate=True).then_inc(s_max[b], 1)

            def rowinv(b, n):
                i = NT - 1 - n
                dve.wait_ge(p_ready[b], n + 1)
                v.reciprocal(rowinv_sb[:, b, i:i + 1], rowsum[:, b, i:i + 1]).then_inc(inv_ready[b], 1)

            def residual1(b, n):
                i = NT - 1 - n
                dve.wait_ge(inv_ready[b], n + 1)
                dve.wait_ge(o_mm[b], n + 1)
                v.scalar_tensor_tensor(x1[b][:, i, :], T[b][:, i * P:(i + 1) * P],
                                       rowinv_sb[:, b, i:i + 1], x_sb[b][:, i, :], ALU.mult,
                                       ALU.add).then_inc(x1_ready[b], 1)

            def stats1(b, n):
                dve.wait_ge(x1_ready[b], n + 1)
                row_stats(1, b, NT - 1 - n, x1[b])

            def query_lo(b, j):
                dve.wait_ge(q_hi[b], j + 1)
                v.scalar_tensor_tensor(r(q_split[b][j][GR:2 * GR, :]),
                                       (V, W)[vw_use["query", b, j] % 2][b][GR:2 * GR, :],
                                       crossw[GR:2 * GR, X_BQ + j:X_BQ + j + 1],
                                       q_split[b][j][GR:2 * GR, :], ALU.add, ALU.subtract
                                       ).then_inc(vw_read[b], 1)

            def rowmax2(b, at):
                n, j, i = vw_use["scores2", b, at], at // NT, at % NT
                dve.wait_ge(s2_mm[b], at + 1)
                v.tensor_reduce(max2[:, b, j, i, :],
                                (V, W)[n % 2][b][:, 0:GK].rearrange("p (h t) -> p h t", h=HG), AX.X,
                                ALU.max, negate=True).then_inc(vw_read[b], 1)

            def max_split(b, j):
                dve.wait_ge(vw_read[b], vw_use["scores2", b, NT * j + NT - 1] + 1)
                hi, lo = max2_split[:, b, j, :, 0:HG], max2_split[:, b, j, :, HG:MR]
                link(v.tensor_copy(r(hi), max2[:, b, j, :, :]))
                v.tensor_tensor(r(lo), max2[:, b, j, :, :], hi, ALU.subtract).then_inc(m_split[b], 1)

            def den_inverse(b, _):
                dve.wait_ge(dT_mm[b], 1)
                link(v.reciprocal(den_inv[:, b, :, :],
                                  W[b][:, :].rearrange("p (t h d) -> p t h d", t=NT, d=HD)[:, :, :, 0]))
                v.tensor_copy(den_inv8[b][:, :, :].rearrange("p t (h d) -> p t h d", d=HD),
                              den_inv[:, b, :, :].unsqueeze(3).broadcast_to([P, NT, NH, HD])
                              ).then_inc(dinv_ready[b], 1)

            def y_scale(b, _):
                dve.wait_ge(rT_mm[b], 1)
                dve.wait_ge(num_ready[b], 1)
                v.tensor_tensor(yT[b][:, :], num_sb[b][:, :], W[b][:, :], ALU.mult).then_inc(yT_ready[b], 1)

            def residual2(b, _):
                dve.wait_ge(wp_mm[b], 1)
                dve.wait_ge(x1b_ready[b], 1)
                v.tensor_tensor(x2[b][:, :, :], x1b[b][:, :, :],
                                V[b][:, :].rearrange("p (t d) -> p t d", d=D), ALU.add).then_inc(x2_ready[b], 1)

            def t_lo(b, _):
                dve.wait_ge(tT_hi_ready[b], 1)
                v.tensor_tensor(r(tT_lo[b][:, :]), T[b][:, :], tT_hi[b][:, :],
                                ALU.subtract).then_inc(tT_lo_ready[b], 1)

            def router_gate(b, _):
                dve.wait_ge(rout_tanh[b], 1)
                dve.wait_ge(rout_z[b], 1)
                v.scalar_tensor_tensor(routT[b][:, :], router_th[b][:, :], 1.0, router_z[b][:, :], ALU.add,
                                       ALU.mult).then_inc(rout_ready[b], 1)

            def top2(b, part):
                lg = logits[:, b]
                if part == 0:
                    dve.wait_ge(d_ffn, 16)
                    dve.wait_ge(lg_mm[b], 1)
                    link(v.scalar_tensor_tensor(
                        lg, V[b][:, 0:NT * NE].rearrange("p (t e) -> p t e", e=NE), 0.5,
                        ffnw[:, F_RB2:F_RB2 + NE].unsqueeze(1).broadcast_to([P, NT, NE]), ALU.mult, ALU.add))
                    for t in range(NT):
                        mark(v.max(top8[:, b, t, :], lg[:, t, :]))
                    dve.wait_ge(dve_step, steps[0])
                    v.tensor_tensor(gap[:, b, :], top8[:, b, :, 1], top8[:, b, :, 0],
                                    ALU.subtract).then_inc(gap_ready[b], 1)
                    for t in range(NT):
                        mark(v.max_index(top8_at[:, b, t, :], top8[:, b, t, :], lg[:, t, :]))
                    dve.wait_ge(dve_step, steps[0])
                    mark(v.tensor_copy(top_at[:, b, :, :], top8_at[:, b, :, 0:TOPK]))
                    return
                dve.wait_ge(dve_step, steps[0])
                for k in range(TOPK):
                    mark(v.tensor_tensor(w_hot[:, b, k], cst[:, C_IOTA:C_IOTA + NE].unsqueeze(1)
                                         .broadcast_to([P, NT, NE]),
                                         top_at[:, b, :, k].unsqueeze(2).broadcast_to([P, NT, NE]),
                                         ALU.is_equal))
                dve.wait_ge(tanh_ready[b], 1)
                for k in range(TOPK):
                    mark(v.tensor_scalar(w_top[:, b, k, :], gap_tanh[:, b, :], (-0.5, 0.5)[k], 0.5,
                                         ALU.mult, ALU.add))
                dve.wait_ge(dve_step, steps[0])
                for k in range(TOPK):
                    mark(v.tensor_tensor(w_part[:, b, k], w_hot[:, b, k],
                                         w_top[:, b, k, :].unsqueeze(2).broadcast_to([P, NT, NE]), ALU.mult))
                dve.wait_ge(dve_step, steps[0])
                v.tensor_tensor(w_all[:, b], w_part[:, b, 0], w_part[:, b, 1], ALU.add).then_inc(w_ready[b], 1)

            def weights_split(b, _):
                dve.wait_ge(wT_full[b], 1)
                v.tensor_copy(r(wT_split[b][0:NE, :]), V[b][0:NE, :]).then_inc(wT_hi[b], 1)
                dve.wait_ge(wT_hi[b], 1)
                v.tensor_tensor(r(wT_split[b][32:32 + NE, :]), V[b][0:NE, :], wT_split[b][0:NE, :],
                                ALU.subtract).then_inc(wT_lo[b], 1)

            def scale(b, u):
                dve.wait_ge(silu_ready[b], u + 1)
                dve.wait_ge(wb_mm[b], u // FC + 1)
                if u >= NS:
                    dve.wait_ge(e_mm[b], u - NS + 1)
                v.tensor_tensor(hidw[b][u % NS][:, :], hid[b][u % NS][:, :], V[b][:, :],
                                ALU.mult).then_inc(hidw_ready[b], 1)

            def add_rows(b, _):
                dve.wait_ge(yo_mm[b], 1)
                dve.wait_ge(res_ready[b], 1)
                v.tensor_tensor(out_sb[b][:, :, :], res[b][:, :, :],
                                T[b][:, :].rearrange("p (t d) -> p t d", d=D), ALU.add).then_inc(out_ready[b], 1)

            parts = dict(norm1=norm1, norm2=norm2, norm3=norm3, val_copy=val_copy, keys_lo=keys_lo,
                         value_rows=value_rows, rowmax1=rowmax1, rowinv=rowinv, residual1=residual1,
                         stats1=stats1, query_lo=query_lo, rowmax2=rowmax2, max_split=max_split,
                         den_inverse=den_inverse, y_scale=y_scale, residual2=residual2, t_lo=t_lo, router_gate=router_gate,
                         top2=top2, weights_split=weights_split, scale=scale, add_rows=add_rows)
            for step, b, i in SCHEDULE:
                if step in parts:
                    parts[step](b, i)

        @block.tensor
        def _(pe):
            mm, tr = nc.tensor.matmul, nc.tensor.transpose

            def cols(i):
                return slice(i * P, (i + 1) * P)

            pe.wait_ge(d_self, 16)
            mm(T[1][:, 0:P], selfw[:, 0:P], selfw[:, P:2 * P], start=True, stop=True)
            mm(T[1][:, P:2 * P], selfw[:, 2 * P:3 * P], selfw[:, 3 * P:4 * P], start=True,
               stop=True).then_inc(aw_mm, 1)
            pe.wait_ge(d_const, 16)

            def x_T(b, stage):
                if stage == 0 and b == 1:
                    pe.wait_ge(aw_ready, 2)
                if stage == 1:
                    pe.wait_ge(x1_ready[b], NT)
                for t in range(NT):
                    pe.wait_ge(norm_ready[b], NT * stage + t + 1)
                    last = tr(T[b][:, cols(t)], xn[b][:, t, :], ident)
                last.then_inc(norm_T_mm[b], 1)

            def context_T(b, _):
                pe.wait_ge(d_ctx, 16)
                for n in range(B):
                    last = tr(W[0][:, n * TC:(n + 1) * TC], ctx_sb[:, n, :], ident[0:TC, 0:TC])
                last.then_inc(ctxT_mm, 1)

            def project1(b, _):
                pe.wait_ge(aw_ready, 2)
                pe.wait_ge(norm_T_ready[b], 1)
                mm(T[b][:, :], a_sb[:, :], xT[b][:, :], start=True, stop=True).then_inc(g_mm[b], 1)
                for t in range(NT):
                    last = mm(U[b][:, cols(t)], xT[b][:, cols(t)], w12[:, :], start=True, stop=True)
                last.then_inc(v_mm[b], 1)

            def keys(b, _):
                pe.wait_ge(d_cross, 16)
                pe.wait_ge(d_bk, 16)
                pe.wait_ge(ctxT_ready, B)
                for j in range(NG):
                    k_out = W[b][0:QR, j * TC:(j + 1) * TC]
                    mm(k_out, crossw[:, X_WK + j * QR:X_WK + (j + 1) * QR], ctxT[:, b, 0, :], start=True,
                       stop=False)
                    last = mm(k_out, bkrow[0:1, j * QR:(j + 1) * QR], bkrow[0:1, NG * QR:NG * QR + TC],
                              start=False, stop=True)
                last.then_inc(k_mm[b], 1)

            def values(b, _):
                flat = ctxT[:, b, :, :].rearrange("p h t -> p (h t)")
                for c in range(NC):
                    last = mm(V[b][0:CROWS[c], cols(c)], flat[:, c * CR:c * CR + CROWS[c]],
                              crossw[:, X_WV:X_WV + D], start=True, stop=True)
                last.then_inc(v2_mm[b], 1)

            def scores1(b, n):
                i = NT - 1 - n
                if n == 0:
                    pe.wait_ge(mask_ready, 2)
                    pe.wait_ge(g_ready[b], 1)
                    pe.wait_ge(v2_rows[b], NC)
                elif n == 1:
                    pe.wait_ge(v_ready[b], 1)
                else:
                    pe.wait_ge(p_ready[b], n - 1)
                sc = (V, U)[n % 2][b]
                mm(sc[:, 0:(i + 1) * P], gT[b][:, cols(i)], xT[b][:, 0:(i + 1) * P], start=True, stop=False)
                mm(sc[:, cols(i)], ident_b[:, :], causal_b[:, :], start=False, stop=True).then_inc(s_mm[b], 1)

            def probs_T(b, n):
                i = NT - 1 - n
                pe.wait_ge(p_ready[b], n + 1)
                if n > 0:
                    pe.wait_ge(pT_ready[b], n)
                else:
                    pe.wait_ge(k_lo[b], 1)
                for k in range(i + 1):
                    last = tr(W[b][:, cols(k)], prob[b][i][:, cols(k)], ident)
                last.then_inc(pT_mm[b], 1)

            def attend1(b, n):
                i = NT - 1 - n
                if n == 0:
                    pe.wait_ge(g_ready[b], 1)
                else:
                    pe.wait_ge(x1_ready[b], n)
                pe.wait_ge(pT_ready[b], n + 1)
                for k in range(i + 1):
                    last = mm(T[b][:, cols(i)], probT[b][i][:, cols(k)], val[b][:, k, :],
                              start=(k == 0), stop=(k == i))
                last.then_inc(o_mm[b], 1)

            def query(b, j):
                n = vw_use["query", b, j]
                if n >= 2:
                    pe.wait_ge(vw_read[b], n - 1)
                elif n == 0:
                    pe.wait_ge(p_ready[b], NT)
                    pe.wait_ge(norm_T_ready[b], 2)
                else:
                    pe.wait_ge(pT_ready[b], NT)
                mm((V, W)[n % 2][b][0:QR, :], crossw[:, X_WQ + j * QR:X_WQ + (j + 1) * QR], xT[b][:, :],
                   start=True, stop=True).then_inc(q_mm[b], 1)

            def scores2(b, at):
                n, j, i = vw_use["scores2", b, at], at // NT, at % NT
                pe.wait_ge(vw_read[b], vw_use["query", b, j] + 1)
                pe.wait_ge(vw_read[b], n - 1)
                pe.wait_ge(k_ready[b], j + 1)
                mm((V, W)[n % 2][b][:, 0:GK], r(q_split[b][j][0:QR, cols(i)]), r(k_diag[b][0:QR, j, :]),
                   start=True, stop=True).then_inc(s2_mm[b], 1)

            def maxima_T(b, j):
                n = tu_use["maxima_T", b, j]
                pe.wait_ge(m_split[b], j + 1)
                if n >= 3:
                    pe.wait_ge(tu_read[b], n - 2)
                for i in range(NT):
                    last = tr((T, U)[n % 2][b][0:MR, cols(i)], max2_split[:, b, j, i, :], ident)
                last.then_inc(tu_mm[b], 1)

            def keyscores2(b, at):
                n, j, c = tu_use["keyscores2", b, at], at // NC, at % NC
                if n >= 3:
                    pe.wait_ge(tu_read[b], n - 2)
                pe.wait_ge(tu_read[b], tu_use["maxima_T", b, j])
                mm((T, U)[n % 2][b][0:CROWS[c], :], r(k_diag[b][:, j, c * CR:c * CR + CROWS[c]]),
                   r(q_split[b][j][:, :]), start=True, stop=True).then_inc(tu_mm[b], 1)

            def attend2(b, part):
                c, dst = part % NC, (W, V)[part // NC]
                if part == 0:
                    pe.wait_ge(ones_ready, 1)
                    pe.wait_ge(vw_read[b], NG + NG * NT)
                    pe.wait_ge(tu_read[b], NG + NG * NC)
                if part == NC:
                    pe.wait_ge(v2_ready[b], NC)
                k = CROWS[c]
                for j in range(NG):
                    lhsT = v_diag[b][0:k, c, j * GR:(j + 1) * GR] if dst is V else ones_diag[0:k, c, :]
                    last = mm(dst[b][j * GR:(j + 1) * GR, :], lhsT, prob2[b][j * NC + c][0:k, :],
                              start=(c == 0), stop=(c == NC - 1), tile_position=(0, j * GR))
                if c == NC - 1:
                    last.then_inc((den_mm, num_mm)[part // NC][b], 1)

            def den_T(b, _):
                pe.wait_ge(den_ready[b], 1)
                for i in range(NT):
                    last = tr(W[b][:, cols(i)], den_sb[b][:, cols(i)], ident)
                last.then_inc(dT_mm[b], 1)

            def den_back(b, _):
                pe.wait_ge(dinv_ready[b], 1)
                for i in range(NT):
                    last = tr(W[b][:, cols(i)], den_inv8[b][:, i, :], ident)
                last.then_inc(rT_mm[b], 1)

            def project(b, _):
                pe.wait_ge(yT_ready[b], 1)
                for i in range(NT):
                    last = mm(V[b][:, cols(i)], yT[b][:, cols(i)], crossw[:, X_WP:X_WP + D], start=True,
                              stop=True)
                last.then_inc(wp_mm[b], 1)

            def router(b, _):
                pe.wait_ge(d_ffn, 16)
                pe.wait_ge(norm_T_ready[b], 3)
                mm(U[b][:, :], ffnw[:, F_RW1:F_RW1 + P], tT[b][:, :], start=True, stop=True).then_inc(hid_mm[b], 1)

            def logits_(b, _):
                pe.wait_ge(rout_ready[b], 1)
                pe.wait_ge(x2_ready[b], 1)
                for t in range(NT):
                    last = mm(V[b][:, t * NE:(t + 1) * NE], routT[b][:, cols(t)], ffnw[:, F_RW2:F_RW2 + NE],
                              start=True, stop=True)
                last.then_inc(lg_mm[b], 1)

            def weights_T(b, _):
                pe.wait_ge(w_ready[b], 1)
                for t in range(NT):
                    last = tr(V[b][0:NE, cols(t)], w_all[:, b, t, :], ident)
                last.then_inc(wT_mm[b], 1)

            def hidden(b, u):
                e, c = u // FC, u % FC
                h = slice(c * P, (c + 1) * P)
                if u == 0:
                    pe.wait_ge(tT_lo_ready[b], 1)
                elif u == 1:
                    pe.wait_ge(rout_z[b], 1)
                else:
                    pe.wait_ge(silu_ready[b], u - 1)
                pe.wait_ge(w1_ready, e + 1)
                z = (T, U)[u % 2][b][:, :]
                mm(z, r(w1_hi[:, e, h]), r(tT_hi[b][:, :]), start=True, stop=False)
                mm(z, r(w1_lo[:, e, h]), r(tT_hi[b][:, :]), start=False, stop=False)
                mm(z, r(w1_hi[:, e, h]), r(tT_lo[b][:, :]), start=False, stop=True).then_inc(z_mm[b], 1)

            def weight_row(b, e):
                if e == 0:
                    pe.wait_ge(pick_ready, 1)
                    pe.wait_ge(wT_lo[b], 1)
                    pe.wait_ge(d_eb2, 16)
                    mm(W[b][:, :], eb2_sb[:, :], wT[b][0:NE, :], start=True, stop=False)
                else:
                    pe.wait_ge(hidw_ready[b], FC * e)
                mm(V[b][:, :], r(pick[:, e:e + 1]).broadcast_to([32 + NE, P]), r(wT_split[b][:, :]), start=True,
                   stop=True).then_inc(wb_mm[b], 1)

            def expert(b, u):
                e, c = u // FC, u % FC
                pe.wait_ge(d_ew2, 16)
                pe.wait_ge(hidw_ready[b], u + 1)
                mm(W[b][:, :], w2_sb[:, e, c, :], hidw[b][u % NS][:, :], start=False,
                   stop=(u == NU - 1)).then_inc(e_mm[b], 1)

            def finish(b, _):
                pe.wait_ge(y_ready[b], 1)
                for i in range(NT):
                    last = tr(T[b][:, cols(i)], y_sb[b][:, cols(i)], ident)
                last.then_inc(yo_mm[b], 1)

            parts = dict(x_T=x_T, t_T=x_T, context_T=context_T, project1=project1, keys=keys,
                         values=values, scores1=scores1, probs_T=probs_T, attend1=attend1, query=query,
                         scores2=scores2, maxima_T=maxima_T, keyscores2=keyscores2, attend2=attend2,
                         den_T=den_T, den_back=den_back, project=project, router=router, logits=logits_,
                         weights_T=weights_T, hidden=hidden, weight_row=weight_row, expert=expert,
                         finish=finish)
            for step, b, i in SCHEDULE:
                if step in parts:
                    parts[step](b, i)


def kernel(**inputs):
    import numpy as np
    import concourse.bacc as bacc
    from concourse.bass_utils import run_bass_kernel_spmd

    a = {k: np.ascontiguousarray(v) for k, v in inputs.items()}
    row = np.arange(P)
    causal = np.where(row[None, :] > row[:, None], MASKED, 0.0)
    hrow = np.where(row < QR, (row % GR) // HD, (row - QR) % HG)
    hmask = hrow[:, None] == np.arange(HG)[None, :]
    pair = np.arange(NC)[None, :] * CR + row[:, None]
    vmask = ((pair // TC)[:, :, None] == np.arange(HG)[None, None, :]).reshape(P, NC * HG)
    iota = np.tile(np.arange(NE)[None, :], (P, 1))
    pick = (row % 32)[:, None] == np.arange(NE)[None, :]
    consts = np.concatenate([np.eye(P), causal, hmask, vmask, iota, pick], 1).astype(np.float32)

    def rep(w):
        parts = [w[..., j * GR:(j + 1) * GR] for j in range(NG) for _ in range(REPS)]
        return np.concatenate(parts, -1)

    def across(v):
        return np.tile(v[None, :], (P, 1))

    self_w = np.concatenate([a["L0_attn_w_q"].T, a["L0_attn_w_k"].T, a["L0_attn_w_v1"].T,
                             a["L0_attn_w_v2"]], 1)
    bq = np.concatenate([rep(a["L0_xattn_bq"]).reshape(NG, QR).T, np.zeros((P - QR, NG), np.float32)], 0)
    cross_w = np.concatenate([rep(a["L0_xattn_Wq"].T), rep(a["L0_xattn_Wk"].T), a["L0_xattn_Wv"].T,
                              a["L0_xattn_Wp"].T, bq, across(a["L0_xattn_bv"]), across(a["L0_xattn_bp"])], 1)
    bk_row = np.concatenate([rep(a["L0_xattn_bk"]), np.ones(TC, np.float32)])[None, :]
    ffn_w = np.concatenate([a["L0_ffn_rw1"], a["L0_ffn_rw2"], a["L0_ffn_rb1"][:, None],
                            a["L0_ffn_eb1"].reshape(NU, P).T, across(a["L0_ffn_rb2"])], 1)
    arrays = {"x": a["x"], "ctx": a["ctx_1024"], "consts": consts, "self_w": self_w, "cross_w": cross_w,
              "bk_row": bk_row, "ffn_w": ffn_w, "eb2": a["L0_ffn_eb2"], "ew1": a["L0_ffn_ew1"],
              "ew2": a["L0_ffn_ew2"]}
    arrays = {k: np.ascontiguousarray(v) for k, v in arrays.items()}
    nc = bacc.Bacc("TRN2", target_bir_lowering=False, num_devices=1)
    aps = [nc.dram_tensor(f"in_{k}", v.shape, mybir.dt.float32, kind="ExternalInput").ap()
           for k, v in arrays.items()]
    out = nc.dram_tensor("out", (B, S, D), mybir.dt.float32, kind="ExternalOutput").ap()
    decoder_block(nc, *aps, out)
    result = run_bass_kernel_spmd(nc, [{f"in_{k}": v for k, v in arrays.items()}], core_ids=[0])
    return result.results[0]["out"]
```

```python
import concourse.bass as bass
from concourse import mybir

B, S, D = 2, 512, 128
P = 128
NT = S // P
KD = 64
TC = 77
NH, HD = 16, 8
HG = 4
NG = NH // HG
GR = HG * HD
REPS = 3
QR = REPS * GR
MR = 2 * HG
GK = HG * TC
NC = 3
CR = -(-GK // NC)
CROWS = [min(CR, GK - c * CR) for c in range(NC)]
NE, FH, TOPK = 8, 256, 2
FC = FH // P
NU = NE * FC
EPS = 1e-5
MASKED = -3.0e38
ROOT_OPS = 3 + 3 * 3
POOL_LO = 3
NHID = 6
EPB = S // FH
PT_AT = [P * n * (n + 1) // 2 for n in range(NT + 1)]
PT_END = PT_AT[-1]
TENSOR_STEPS = """
context_T.0.0 keys.0.0 values.0.0 x_T.0.0 keys.1.0 project1.0.0 scores1.0.0 values.1.0 x_T.1.0
scores1.0.1 probs_T.0.0 project1.1.0 scores1.0.2 scores1.1.0 attend1.0.0 probs_T.0.1 scores1.0.3
scores1.1.1 probs_T.1.0 attend1.0.1 probs_T.0.2 scores1.1.2 attend1.0.2 probs_T.0.3 attend1.1.0
scores1.1.3 attend1.0.3 probs_T.1.1 x_T.0.1 attend1.1.1 query.0.0 probs_T.1.2 query.0.1 query.0.2
attend1.1.2 query.0.3 probs_T.1.3 scores2.0.0 scores2.0.1 attend1.1.3 scores2.0.2 scores2.0.3
scores2.0.4 scores2.0.5 scores2.0.6 maxima_T.0.0 scores2.0.7 scores2.0.8 keyscores2.0.0 keyscores2.0.1
scores2.0.9 x_T.1.1 maxima_T.0.1 scores2.0.10 keyscores2.0.2 scores2.0.11 keyscores2.0.3 scores2.0.12
keyscores2.0.4 scores2.0.13 query.1.0 query.1.1 scores2.0.14 maxima_T.0.2 keyscores2.0.5 scores2.0.15
query.1.2 query.1.3 keyscores2.0.6 scores2.1.0 keyscores2.0.7 scores2.1.1 maxima_T.0.3 scores2.1.2
keyscores2.0.8 scores2.1.3 keyscores2.0.9 scores2.1.4 keyscores2.0.10 scores2.1.5 maxima_T.1.0
scores2.1.6 keyscores2.0.11 scores2.1.7 keyscores2.1.0 keyscores2.1.1 scores2.1.8 scores2.1.9
attend2.0.0 attend2.0.1 attend2.0.2 maxima_T.1.1 scores2.1.10 keyscores2.1.2 scores2.1.11 attend2.0.3
keyscores2.1.3 scores2.1.12 keyscores2.1.4 scores2.1.13 attend2.0.4 den_T.0.0 scores2.1.14 scores2.1.15
maxima_T.1.2 keyscores2.1.5 attend2.0.5 den_back.0.0 keyscores2.1.6 keyscores2.1.7 maxima_T.1.3
project.0.0 keyscores2.1.8 keyscores2.1.9 keyscores2.1.10 keyscores2.1.11 attend2.1.0 attend2.1.1
attend2.1.2 t_T.0.2 router.0.0 attend2.1.3 hidden.0.0 hidden.0.1 logits.0.0 attend2.1.4 weights_T.0.0
attend2.1.5 den_T.1.0 hidden.0.2 weight_row.0.0 hidden.0.3 den_back.1.0 weight_row.0.1 expert.0.0
hidden.0.4 project.1.0 expert.0.1 weight_row.0.2 hidden.0.5 hidden.0.6 expert.0.2 expert.0.3
weight_row.0.3 expert.0.4 hidden.0.7 hidden.0.8 weight_row.0.4 hidden.0.9 expert.0.5 expert.0.6
hidden.0.10 t_T.1.2 expert.0.7 router.1.0 hidden.0.11 weight_row.0.5 expert.0.8 hidden.0.12 hidden.1.0
logits.1.0 expert.0.9 weight_row.0.6 expert.0.10 hidden.0.13 expert.0.11 hidden.0.14 weights_T.1.0
hidden.0.15 hidden.1.1 expert.0.12 weight_row.0.7 weight_row.1.0 hidden.1.2 expert.0.13 hidden.1.3
weight_row.1.1 expert.1.0 hidden.1.4 expert.1.1 hidden.1.5 expert.0.14 weight_row.1.2 hidden.1.6
expert.1.2 expert.0.15 hidden.1.7 expert.1.3 weight_row.1.3 hidden.1.8 expert.1.4 expert.1.5 hidden.1.9
weight_row.1.4 expert.1.6 hidden.1.10 hidden.1.11 expert.1.7 weight_row.1.5 expert.1.8 hidden.1.12
finish.0.0 finish.0.1 expert.1.9 weight_row.1.6 hidden.1.13 hidden.1.14 expert.1.10 expert.1.11
weight_row.1.7 hidden.1.15 expert.1.12 expert.1.13 expert.1.14 expert.1.15 finish.1.0 finish.1.1"""
SCALAR_STEPS = """
context_copy.0.0 keys_hi.0.0 x_copy.0.0 keys_hi.1.0 g_copy.0.0 exp1.0.0 x_copy.1.0 probs_copy.0.0
exp1.0.1 g_copy.1.0 exp1.0.2 exp1.1.0 probs_copy.0.1 exp1.0.3 exp1.1.1 probs_copy.0.2 probs_copy.1.0
exp1.1.2 probs_copy.0.3 probs_copy.1.1 x_copy.0.1 query_hi.0.0 probs_copy.1.2 query_hi.0.1 exp1.1.3
query_hi.0.2 query_hi.0.3 probs_copy.1.3 maxima_row.0.0 exp2.0.0 exp2.0.1 maxima_row.0.1 exp2.0.2
x_copy.1.1 exp2.0.3 exp2.0.4 query_hi.1.0 query_hi.1.1 maxima_row.0.2 exp2.0.5 query_hi.1.2 query_hi.1.3
exp2.0.6 exp2.0.7 maxima_row.0.3 exp2.0.8 exp2.0.9 exp2.0.10 maxima_row.1.0 exp2.0.11 exp2.1.0 exp2.1.1
den_copy.0.0 maxima_row.1.1 exp2.1.2 exp2.1.3 exp2.1.4 maxima_row.1.2 exp2.1.5 num_copy.0.0 exp2.1.6
exp2.1.7 maxima_row.1.3 exp2.1.8 exp2.1.9 exp2.1.10 exp2.1.11 t_copy.0.2 router_tanh.0.0 silu.0.0
den_copy.1.0 tanh.0.0 weights_copy.0.0 silu.0.1 weighted_hi.0.0 num_copy.1.0 silu.0.2 weighted_hi.0.1
silu.0.3 silu.0.4 weighted_hi.0.2 weighted_hi.0.3 silu.0.5 weighted_hi.0.4 weighted_hi.0.5 silu.0.6
silu.0.7 silu.0.8 weighted_hi.0.6 weighted_hi.0.7 silu.0.9 t_copy.1.2 weighted_hi.0.8 silu.0.10
weighted_hi.0.9 router_tanh.1.0 silu.0.11 weighted_hi.0.10 silu.1.0 silu.0.12 weighted_hi.0.11 tanh.1.0
silu.0.13 weighted_hi.0.12 weights_copy.1.0 silu.0.14 silu.1.1 weighted_hi.0.13 silu.0.15 silu.1.2
weighted_hi.1.0 weighted_hi.1.1 weighted_hi.0.14 silu.1.3 weighted_hi.1.2 silu.1.4 weighted_hi.1.3
silu.1.5 weighted_hi.0.15 weighted_hi.1.4 silu.1.6 weighted_hi.1.5 silu.1.7 y_copy.0.0 silu.1.8
weighted_hi.1.6 weighted_hi.1.7 silu.1.9 weighted_hi.1.8 silu.1.10 y_copy.0.1 weighted_hi.1.9 silu.1.11
weighted_hi.1.10 silu.1.12 weighted_hi.1.11 silu.1.13 silu.1.14 weighted_hi.1.12 weighted_hi.1.13
silu.1.15 weighted_hi.1.14 weighted_hi.1.15 y_copy.1.0 y_copy.1.1"""
VECTOR_STEPS = """
norm1.0.0 norm1.0.1 keys_full.0.0 keys_lo.0.0 value_rows.0.0 norm1.1.1 keys_full.1.0 val_copy.0.0
keys_lo.1.0 rowmax1.0.0 rowmax1.0.1 value_rows.1.0 val_copy.1.0 rowmax1.0.2 rowmax1.1.0 rowinv.0.0
residual1.0.0 rowinv.1.0 stats1.0.0 rowmax1.0.3 rowmax1.1.1 rowinv.0.1 residual1.0.1 stats1.0.1
rowinv.0.2 rowmax1.1.2 residual1.0.2 stats1.0.2 residual1.1.0 stats1.1.0 rowinv.0.3 residual1.0.3
stats1.0.3 norm2.0.0 norm2.0.1 norm2.0.2 norm2.0.3 norm2.0.4 norm2.0.5 norm2.0.6 norm2.0.7 norm2.0.8
norm2.0.9 norm2.0.10 norm2.0.11 norm2.0.12 rowinv.1.1 norm2.0.13 residual1.1.1 query_lo.0.0 rowmax1.1.3
rowinv.1.2 query_lo.0.1 stats1.1.1 query_lo.0.2 residual1.1.2 query_lo.0.3 stats1.1.2 rowmax2.0.0
rowmax2.0.1 rowinv.1.3 residual1.1.3 rowmax2.0.2 stats1.1.3 rowmax2.0.3 max_split.0.0 rowmax2.0.4
norm2.1.0 norm2.1.1 norm2.1.2 norm2.1.3 rowmax2.0.5 norm2.1.4 norm2.1.5 norm2.1.6 norm2.1.7 rowmax2.0.6
norm2.1.8 norm2.1.9 norm2.1.10 norm2.1.11 rowmax2.0.7 norm2.1.12 norm2.1.13 max_split.0.1 rowmax2.0.8
rowmax2.0.9 rowmax2.0.10 rowmax2.0.11 max_split.0.2 rowmax2.0.12 rowmax2.0.13 query_lo.1.0 query_lo.1.1
rowmax2.0.14 rowmax2.0.15 max_split.0.3 query_lo.1.2 query_lo.1.3 rowmax2.1.0 rowmax2.1.1 rowmax2.1.2
rowmax2.1.3 max_split.1.0 rowmax2.1.4 rowmax2.1.5 rowmax2.1.6 rowmax2.1.7 rowmax2.1.8 max_split.1.1
rowmax2.1.9 rowmax2.1.10 rowmax2.1.11 max_split.1.2 rowmax2.1.12 rowmax2.1.13 den_inverse.0.0
rowmax2.1.14 rowmax2.1.15 max_split.1.3 y_scale.0.0 residual2.0.0 norm3.0.0 norm3.0.1 norm3.0.2
norm3.0.3 norm3.0.4 norm3.0.5 norm3.0.6 norm3.0.7 norm3.0.8 norm3.0.9 norm3.0.10 norm3.0.11 norm3.0.12
norm3.0.13 t_lo.0.0 router_gate.0.0 top2.0.0 top2.0.1 weights_split.0.0 den_inverse.1.0 scale.0.0
scale.0.1 weighted_lo.0.0 y_scale.1.0 scale.0.2 weighted_lo.0.1 scale.0.3 residual2.1.0 scale.0.4
weighted_lo.0.3 scale.0.5 weighted_lo.0.4 norm3.1.0 norm3.1.1 scale.0.6 norm3.1.2 norm3.1.3 norm3.1.4
norm3.1.5 scale.0.7 norm3.1.6 weighted_lo.0.6 norm3.1.7 norm3.1.8 norm3.1.9 norm3.1.10 norm3.1.11
norm3.1.12 norm3.1.13 scale.0.8 weighted_lo.0.7 scale.0.9 t_lo.1.0 scale.0.10 router_gate.1.0
weighted_lo.0.9 scale.0.11 weighted_lo.0.10 top2.1.0 scale.0.12 top2.1.1 scale.0.13 weighted_lo.0.12
weights_split.1.0 scale.0.14 weighted_lo.0.13 scale.1.0 scale.1.1 scale.0.15 weighted_lo.1.0 scale.1.2
weighted_lo.1.1 scale.1.3 weighted_lo.1.3 scale.1.4 weighted_lo.0.15 weighted_lo.1.4 scale.1.5 scale.1.6
scale.1.7 weighted_lo.1.6 scale.1.8 weighted_lo.1.7 scale.1.9 scale.1.10 weighted_lo.1.9 scale.1.11
weighted_lo.1.10 add_rows.0.0 scale.1.12 scale.1.13 add_rows.0.1 weighted_lo.1.12 scale.1.14
weighted_lo.1.13 scale.1.15 weighted_lo.1.15 add_rows.1.0 add_rows.1.1"""
GPSIMD_STEPS = """
weighted_lo_pool.0.2 skip_rows.0.0 weighted_lo_pool.0.5 weighted_lo_pool.0.8 weighted_lo_pool.0.11
weighted_lo_pool.0.14 weighted_lo_pool.1.2 weighted_lo_pool.1.5 weighted_lo_pool.1.8
weighted_lo_pool.1.11 weighted_lo_pool.1.14 skip_rows.1.0"""
NS = 3

C_ID, C_CAUSAL, C_HMASK, C_VMASK, C_IOTA = 0, 128, 256, 260, 272
C_PICK = 280
C_END = 288
X_WQ, X_WK, X_WV, X_WP = 0, 384, 768, 896
X_BQ, X_BV, X_BP, X_BK, X_END = 1024, 1028, 1156, 1284, 1288
F_RW1, F_RW2, F_RB1, F_EB1, F_RB2, F_END = 0, 128, 136, 137, 153, 161


def steps_of(text):
    return [(name, int(b), int(i)) for name, b, i in (word.split(".") for word in text.split())]


def uses(steps, kinds):
    count, use = [0] * B, {}
    for step, b, i in steps:
        if step in kinds:
            use[step, b, i] = count[b]
            count[b] += 1
    return use


def decoder_block(nc, x, ctx, consts, self_w, cross_w, ffn_w, eb2, ew1, ew2, out):
    f32, f32r, bf16, u32, i32 = (mybir.dt.float32, mybir.dt.float32r, mybir.dt.bfloat16,
                                 mybir.dt.uint32, mybir.dt.int32)
    ALU, ACT, AX = mybir.AluOpType, mybir.ActivationFunctionType, mybir.AxisListType

    def sb(name, shape, dt=f32):
        return nc.alloc_sbuf_tensor(name, shape, dt)

    def sb2(name, shape, dt=f32):
        return [sb(f"{name}{b}", shape, dt) for b in range(B)]

    def sem(name):
        return nc.alloc_semaphore(name)

    def sem2(name):
        return [sem(f"{name}{b}") for b in range(B)]

    def r(ap):
        return ap.bitcast(f32r)

    x_sb = sb2("x_sb", [P, NT, D])
    cst = sb("cst", [P, C_END])
    ident = cst[:, C_ID:C_ID + P]
    ident_b = sb("ident_b", [P, P], bf16)
    causal_b = sb("causal_b", [P, P], bf16)
    selfw = sb("selfw", [KD, 4 * P])
    crossw = sb("crossw", [P, X_END])
    ffnw = sb("ffnw", [P, F_END])
    eb2_sb = sb("eb2_sb", [NE, D])
    ctx_sb = sb("ctx_sb", [TC, B, D])
    w1_sb = sb("w1_sb", [P, NE, FH])
    w1_hi = sb("w1_hi", [P, NE, FH])
    w1_lo = sb("w1_lo", [P, NE, FH])
    stats = sb("stats", [P, 3, B, NT, 6])
    meanvar = sb("meanvar", [P, 3, B, NT, 2])
    ln_var = sb("ln_var", [P, 3, B, NT])
    ln_half = sb("ln_half", [P, 3, B, NT], i32)
    ln_root = sb("ln_root", [P, 3, 4, B, NT], i32)
    ln_tmp = sb("ln_tmp", [P, 3, 6, B, NT])
    xn = sb2("xn", [P, NT, D])
    a_sb = sb("a_sb", [P, P])
    w12 = sb("w12", [P, P])
    xT = sb2("xT", [P, S])
    gT = sb2("gT", [P, S])
    val = sb2("val", [P, NT, D])
    negmax = sb("negmax", [P, B, NT])
    rowsum = sb("rowsum", [P, B, NT])
    rowinv_sb = sb("rowinv", [P, B, NT])
    prob_all, probT_all = sb2("prob", [P, PT_END]), sb2("probT", [P, PT_END])
    prob, probT = ([[all_tiles[b][:, PT_AT[i]:PT_AT[i + 1]] for i in range(NT)] for b in range(B)]
                   for all_tiles in (prob_all, probT_all))
    x1 = sb2("x1", [P, NT, D])
    x1b = sb2("x1b", [P, NT, D])
    ctxT = sb("ctxT", [P, B, HG, TC])
    k_split = sb2("k_split", [QR + MR, NG, TC])
    k_full = sb2("k_full", [QR, NG, TC])
    k_diag_all = sb2("k_diag", [P, NG * GK])
    k_diag = [k_diag_all[b][0:QR + MR, :].rearrange("p (j k) -> p j k", j=NG) for b in range(B)]
    v_rows = sb2("v_rows", [CR, NC, D])
    v_diag = sb2("v_diag", [CR, NC, D])
    ones_diag = sb("ones_diag", [CR, NC, GR])
    q_split = [[sb(f"q_split{b}_{j}", [P, S]) for j in range(NG)] for b in range(B)]
    max2 = sb("max2", [P, B, NG, NT, HG])
    max2_split = sb("max2_split", [P, B, NG, NT, MR])
    prob2 = [[sb(f"prob2_{b}_{n}", [P, S]) for n in range(NG * NC)] for b in range(B)]
    den_inv = sb("den_inv", [P, B, NT, NH])
    den_sb = [prob[b][NT - 1] for b in range(B)]
    num_sb = [probT[b][NT - 1] for b in range(B)]
    den_inv8, yT = val, gT
    x2 = x1b
    res = x_sb
    tT_hi = sb2("tT_hi", [P, S])
    tT_lo = sb2("tT_lo", [P, S])
    logits = sb("logits", [P, B, NT, NE])
    top8 = sb("top8", [P, B, NT, 8])
    top8_at = sb("top8_at", [P, B, NT, 8], u32)
    top_at = sb("top_at", [P, B, NT, TOPK])
    gap = sb("gap", [P, B, NT])
    gap_tanh = sb("gap_tanh", [P, B, NT])
    w_top = sb("w_top", [P, B, TOPK, NT])
    w_hot = sb("w_hot", [P, B, TOPK, NT, NE])
    w_part = sb("w_part", [P, B, TOPK, NT, NE])
    w_all = sb("w_all", [P, B, NT, NE])
    wT_split = sb2("wT_split", [32 + NE, S])
    pick = sb("pick", [32 + NE, NE])
    tT = [prob2[b][0] for b in range(B)]
    routT = [prob2[b][1] for b in range(B)]
    y_sb = [prob2[b][2] for b in range(B)]
    hid = [prob2[b][3:3 + NHID] for b in range(B)]
    wT = [prob2[b][3 + NHID] for b in range(B)]
    hidw_new = [[sb(f"hidw{b}_{n}", [P, S]) for n in range(2 * (NS - 1))] for b in range(B)]
    hidw_hi = [hidw_new[b][0:NS - 1] + [k_diag_all[b][:, 0:S]] for b in range(B)]
    hidw_lo = [hidw_new[b][NS - 1:] + [k_diag_all[b][:, S:2 * S]] for b in range(B)]
    w2_sb = [tiles[b][:, 0:S] for b in range(B) for tiles in (prob_all, probT_all)]
    w2_hi, w2_lo = q_split
    out_sb = x1
    router_z, router_th = y_sb, [prob2[b][4 + NHID] for b in range(B)]

    bank = [[nc.alloc_psum_tensor(f"bank{b}_{n}", [P, 512], f32) for n in range(4)] for b in range(B)]
    T, U, V, W = ([bank[b][n] for b in range(B)] for n in range(4))

    d_const, d_self, d_ctx, d_cross, d_ffn, d_eb2, d_ew1, d_ew2, d_out = (
        sem(n) for n in ("d_const", "d_self", "d_ctx", "d_cross", "d_ffn", "d_eb2", "d_ew1",
                         "d_ew2", "d_out"))
    d_x = sem2("d_x")
    (dve_step, pool_step, mask_ready, aw_mm, aw_ready, ctxT_mm, ctxT_ready, ones_ready, pick_ready, w1_ready,
     w2_ready) = (
        sem(n) for n in ("dve_step", "pool_step", "mask_ready", "aw_mm", "aw_ready", "ctxT_mm",
                         "ctxT_ready", "ones_ready", "pick_ready", "w1_ready", "w2_ready"))
    norm_ready, norm_T_mm, norm_T_ready = (sem2(n) for n in ("norm_ready", "norm_T_mm", "norm_T_ready"))
    g_mm, g_ready, v_mm, v_ready = (sem2(n) for n in ("g_mm", "g_ready", "v_mm", "v_ready"))
    k_mm, k_full_ready, k_hi, k_lo, k_ready = (
        sem2(n) for n in ("k_mm", "k_full_ready", "k_hi", "k_lo", "k_ready"))
    v2_mm, v2_rows, v2_ready = (sem2(n) for n in ("v2_mm", "v2_rows", "v2_ready"))
    s_mm, s_max, p_ready = (sem2(n) for n in ("s_mm", "s_max", "p_ready"))
    pT_mm, pT_ready, o_mm, x1_ready, x1b_ready = (
        sem2(n) for n in ("pT_mm", "pT_ready", "o_mm", "x1_ready", "x1b_ready"))
    inv_ready, stat_ready = (sem2(n) for n in ("inv_ready", "stat_ready"))
    q_mm, q_hi, vw_read = (sem2(n) for n in ("q_mm", "q_hi", "vw_read"))
    s2_mm, m_split, tu_mm, tu_read = (sem2(n) for n in ("s2_mm", "m_split", "tu_mm", "tu_read"))
    sums_mm, sums_ready, dT_mm, dinv_ready, rT_mm, yT_ready, wp_mm, x2_ready = (
        sem2(n) for n in ("sums_mm", "sums_ready", "dT_mm", "dinv_ready", "rT_mm", "yT_ready",
                          "wp_mm", "x2_ready"))
    (res_ready, tT_hi_ready, tT_lo_ready, rout_tanh, rout_z, hid_mm, rout_ready, lg_mm, lg_ready, gap_ready,
     tanh_ready) = (sem2(n) for n in (
        "res_ready", "tT_hi_ready", "tT_lo_ready", "rout_tanh", "rout_z", "hid_mm", "rout_ready", "lg_mm",
        "lg_ready", "gap_ready", "tanh_ready"))
    w_ready, wT_mm, wT_full, wT_ready = (
        sem2(n) for n in ("w_ready", "wT_mm", "wT_full", "wT_ready"))
    (wb_mm, z_mm, silu_ready, hidw_ready, hidw_hi_ready, hidw_lo_ready, hidw_lo_pool, e_mm, y_ready, yo_mm,
     out_ready) = (sem2(n) for n in (
        "wb_mm", "z_mm", "silu_ready", "hidw_ready", "hidw_hi_ready", "hidw_lo_ready", "hidw_lo_pool",
        "e_mm", "y_ready", "yo_mm", "out_ready"))

    def lo_done(b, u):
        by_pool = (u + 1) // POOL_LO
        return (hidw_lo_pool[b], by_pool) if (u + 1) % POOL_LO == 0 else (hidw_lo_ready[b], u + 1 - by_pool)

    vw_use = uses(steps_of(TENSOR_STEPS), ("query", "scores2"))
    tu_use = {at: n + 1 for at, n in uses(steps_of(TENSOR_STEPS), ("maxima_T", "keyscores2")).items()}
    x_rows = x.rearrange("b (t p) d -> p b t d", p=P)
    out_rows = out.rearrange("b (t p) d -> p b t d", p=P)

    with nc.Block() as block:

        @block.sync
        def _(sp):
            sp.dma_start(x_sb[0][:, :, :], x_rows[:, 0]).then_inc(d_x[0], 16)
            sp.dma_start(cst[:, :], consts).then_inc(d_const, 16)
            sp.dma_start(x_sb[1][:, :, :], x_rows[:, 1]).then_inc(d_x[1], 16)
            sp.dma_start(w1_sb[:, :, :], ew1.rearrange("e d h -> d e h")).then_inc(d_ew1, 16)
            sp.dma_start(ffnw[:, :], ffn_w).then_inc(d_ffn, 16)
            sp.dma_start(eb2_sb[:, :], eb2).then_inc(d_eb2, 16)
            for b in range(B):
                sp.wait_ge(pT_ready[b], NT)
                sp.wait_ge(x1_ready[b], NT)
                for n in (2 * b, 2 * b + 1):
                    sp.dma_start(w2_sb[n].rearrange("p (e c d) -> p e c d", c=FC, d=D),
                                 ew2[n * EPB:(n + 1) * EPB].rearrange("e (c h) d -> h e c d", h=P)
                                 ).then_inc(d_ew2, 16)
            for b in range(B):
                for half in range(2):
                    at = slice(half * NT // 2, (half + 1) * NT // 2)
                    sp.wait_ge(out_ready[b], half + 1)
                    sp.dma_start(out_rows[:, b, at], out_sb[b][:, at, :]).then_inc(d_out, 16)
            sp.wait_ge(d_out, 16 * 2 * B)

        @block.gpsimd
        def _(pool):
            g = nc.gpsimd
            steps = [0]

            def link(ins):
                steps[0] += 1
                ins.then_inc(pool_step, 1)
                pool.wait_ge(pool_step, steps[0])

            for b in range(B):
                link(g.memset(k_split[b][QR:QR + MR, :, :], 1.0))
            for b in range(B):
                link(g.memset(wT_split[b][:, :], 0.0))
            pool.wait_ge(d_const, 16)
            g.tensor_copy(ident_b[:, :], ident).then_inc(mask_ready, 1)
            g.tensor_copy(causal_b[:, :], cst[:, C_CAUSAL:C_CAUSAL + P]).then_inc(mask_ready, 1)
            vmask = cst[0:CR, C_VMASK:C_VMASK + NC * HG]
            g.tensor_copy(ones_diag[:, :, :].rearrange("p c (h d) -> p (c h) d", d=HD),
                          vmask.unsqueeze(2).broadcast_to([CR, NC * HG, HD])).then_inc(ones_ready, 1)
            hmask = cst[0:QR + MR, C_HMASK:C_HMASK + HG]
            for b in range(B):
                pool.wait_ge(k_lo[b], 1)
                for j in range(NG):
                    g.tensor_tensor(
                        r(k_diag[b][:, j, :]).rearrange("p (h t) -> p h t", h=HG),
                        k_split[b][:, j, :].unsqueeze(1).broadcast_to([QR + MR, HG, TC]),
                        hmask.unsqueeze(2).broadcast_to([QR + MR, HG, TC]), ALU.mult).then_inc(k_ready[b], 1)
            for b in range(B):
                for c in range(NC):
                    k = CROWS[c]
                    pool.wait_ge(v2_rows[b], c + 1)
                    g.tensor_tensor(
                        v_diag[b][0:k, c, :].rearrange("p (j h d) -> p j h d", j=NG, h=HG),
                        v_rows[b][0:k, c, :].rearrange("p (j h d) -> p j h d", j=NG, h=HG),
                        vmask[0:k, c * HG:(c + 1) * HG].unsqueeze(1).unsqueeze(3)
                        .broadcast_to([k, NG, HG, HD]), ALU.mult).then_inc(v2_ready[b], 1)
            g.tensor_copy(r(pick[:, :]), cst[0:32 + NE, C_PICK:C_PICK + NE]).then_inc(pick_ready, 1)
            pool.wait_ge(d_ew1, 16)
            for e in range(NE):
                link(g.tensor_copy(r(w1_hi[:, e, :]), w1_sb[:, e, :]))
                g.tensor_tensor(r(w1_lo[:, e, :]), w1_sb[:, e, :], w1_hi[:, e, :],
                                ALU.subtract).then_inc(w1_ready, 1)
                if e % 4 == 3:
                    b = e // 4
                    pool.wait_ge(x1_ready[b], NT)
                    g.tensor_tensor(x1b[b][:, :, :], x1[b][:, :, :],
                                    crossw[:, X_BP:X_BP + D].unsqueeze(1).broadcast_to([P, NT, D]),
                                    ALU.add).then_inc(x1b_ready[b], 1)
            for b in range(B):
                pool.wait_ge(tu_read[b], NG + NG * NC)
            pool.wait_ge(d_ew2, 16 * len(w2_sb))
            for e in range(NE):
                at = slice(e % EPB * FH, (e % EPB + 1) * FH)
                link(g.tensor_copy(r(w2_hi[e // EPB][:, at]), w2_sb[e // EPB][:, at]))
                g.tensor_tensor(r(w2_lo[e // EPB][:, at]), w2_sb[e // EPB][:, at], w2_hi[e // EPB][:, at],
                                ALU.subtract).then_inc(w2_ready, 1)

            def skip_rows(b, _):
                pool.wait_ge(norm_ready[b], 3 * NT)
                g.tensor_tensor(res[b][:, :, :], x2[b][:, :, :], xn[b][:, :, :], ALU.add).then_inc(res_ready[b], 1)

            def weighted_lo_pool(b, u):
                pool.wait_ge(hidw_hi_ready[b], u + 1)
                g.tensor_tensor(r(hidw_lo[b][u % NS][:, :]), hid[b][u % NHID][:, :], hidw_hi[b][u % NS][:, :],
                                ALU.subtract).then_inc(hidw_lo_pool[b], 1)

            parts = dict(skip_rows=skip_rows, weighted_lo_pool=weighted_lo_pool)
            for step, b, i in steps_of(GPSIMD_STEPS):
                parts[step](b, i)

        @block.scalar
        def _(act):
            a = nc.scalar
            act.dma_start(selfw[:, :], self_w).then_inc(d_self, 16)
            act.dma_start(ctx_sb[:, :, :], ctx.rearrange("b t d -> t b d")).then_inc(d_ctx, 16)
            act.dma_start(crossw[:, :], cross_w).then_inc(d_cross, 16)
            act.wait_ge(aw_mm, 1)
            a.activation(a_sb[:, :], T[1][:, 0:P], ACT.Copy, scale=float(KD) ** -0.5).then_inc(aw_ready, 1)
            a.activation(w12[:, :], T[1][:, P:2 * P], ACT.Copy).then_inc(aw_ready, 1)

            def x_copy(b, stage):
                act.wait_ge(norm_T_mm[b], stage + 1)
                a.activation(xT[b][:, :], T[b][:, :], ACT.Copy).then_inc(norm_T_ready[b], 1)

            def context_copy(b, _):
                act.wait_ge(ctxT_mm, 1)
                for n in range(B):
                    a.activation(ctxT[:, n, :, :], W[0][:, n * TC:(n + 1) * TC].unsqueeze(1)
                                 .broadcast_to([P, HG, TC]), ACT.Copy).then_inc(ctxT_ready, 1)

            def g_copy(b, _):
                act.wait_ge(g_mm[b], 1)
                a.activation(gT[b][:, :], T[b][:, :], ACT.Copy).then_inc(g_ready[b], 1)

            def keys_hi(b, _):
                act.wait_ge(k_full_ready[b], 1)
                a.activation(r(k_split[b][0:QR, :, :]), k_full[b][0:QR, :, :], ACT.Copy).then_inc(k_hi[b], 1)

            def exp1(b, n):
                i = NT - 1 - n
                act.wait_ge(s_max[b], n + 1)
                a.activation(prob[b][i][:, :], (V, U)[n % 2][b][:, 0:(i + 1) * P], ACT.Exp,
                             bias=negmax[:, b, i:i + 1], accum_out=rowsum[:, b, i:i + 1]).then_inc(p_ready[b], 1)

            def probs_copy(b, n):
                i = NT - 1 - n
                act.wait_ge(pT_mm[b], n + 1)
                a.activation(probT[b][i][:, :], W[b][:, 0:(i + 1) * P], ACT.Copy).then_inc(pT_ready[b], 1)

            def query_hi(b, j):
                act.wait_ge(q_mm[b], j + 1)
                a.activation(r(q_split[b][j][0:QR, :]), (V, W)[vw_use["query", b, j] % 2][b][0:QR, :],
                             ACT.Identity, bias=crossw[0:QR, X_BQ + j:X_BQ + j + 1]).then_inc(q_hi[b], 1)

            def maxima_row(b, j):
                n = tu_use["maxima_T", b, j]
                act.wait_ge(tu_mm[b], n)
                a.activation(r(q_split[b][j][QR:QR + MR, :]), (T, U)[n % 2][b][0:MR, :],
                             ACT.Copy).then_inc(tu_read[b], 1)

            def exp2(b, at):
                n, c = tu_use["keyscores2", b, at], at % NC
                act.wait_ge(tu_mm[b], n)
                a.activation(prob2[b][at][0:CROWS[c], :], (T, U)[n % 2][b][0:CROWS[c], :],
                             ACT.Exp, scale=float(HD) ** -0.5).then_inc(tu_read[b], 1)

            def den_copy(b, _):
                act.wait_ge(sums_mm[b], 1)
                a.activation(den_sb[b][:, :], W[b][:, :], ACT.Copy).then_inc(sums_ready[b], 1)

            def num_copy(b, _):
                act.wait_ge(sums_mm[b], 2)
                a.activation(num_sb[b][:, :], V[b][:, :], ACT.Copy).then_inc(sums_ready[b], 1)

            def t_copy(b, stage):
                act.wait_ge(norm_T_mm[b], stage + 1)
                a.activation(tT[b][:, :], T[b][:, :], ACT.Copy).then_inc(norm_T_ready[b], 1)
                a.activation(r(tT_hi[b][:, :]), T[b][:, :], ACT.Copy).then_inc(tT_hi_ready[b], 1)

            def router_tanh(b, _):
                act.wait_ge(d_ffn, 16)
                act.wait_ge(hid_mm[b], 1)
                a.activation(router_z[b][:, :], U[b][:, :], ACT.Identity,
                             bias=ffnw[:, F_RB1:F_RB1 + 1]).then_inc(rout_z[b], 1)
                act.wait_ge(rout_z[b], 1)
                a.activation(router_th[b][:, :], router_z[b][:, :], ACT.Tanh,
                             scale=0.5).then_inc(rout_tanh[b], 1)

            def tanh(b, _):
                act.wait_ge(gap_ready[b], 1)
                a.activation(gap_tanh[:, b, :], gap[:, b, :], ACT.Tanh, scale=0.5).then_inc(tanh_ready[b], 1)

            def weights_copy(b, _):
                act.wait_ge(wT_mm[b], 1)
                a.activation(wT[b][0:NE, :], V[b][0:NE, :], ACT.Copy).then_inc(wT_full[b], 1)

            def silu(b, u):
                act.wait_ge(z_mm[b], u + 1)
                if u >= NHID:
                    act.wait_ge(*lo_done(b, u - NHID))
                a.activation(hid[b][u % NHID][:, :], (T, U)[u % 2][b][:, :], ACT.Silu,
                             bias=ffnw[:, F_EB1 + u:F_EB1 + u + 1]).then_inc(silu_ready[b], 1)

            def weighted_hi(b, u):
                act.wait_ge(hidw_ready[b], u + 1)
                if u >= NS:
                    act.wait_ge(e_mm[b], u - NS + 1)
                a.activation(r(hidw_hi[b][u % NS][:, :]), hid[b][u % NHID][:, :],
                             ACT.Copy).then_inc(hidw_hi_ready[b], 1)

            def y_copy(b, half):
                act.wait_ge(e_mm[b], NU)
                at = slice(half * S // 2, (half + 1) * S // 2)
                a.activation(y_sb[b][:, at], W[b][:, at], ACT.Copy).then_inc(y_ready[b], 1)

            parts = dict(x_copy=x_copy, context_copy=context_copy, g_copy=g_copy, keys_hi=keys_hi, exp1=exp1,
                         probs_copy=probs_copy, query_hi=query_hi, maxima_row=maxima_row, exp2=exp2,
                         den_copy=den_copy, num_copy=num_copy, t_copy=t_copy, router_tanh=router_tanh,
                         tanh=tanh, weights_copy=weights_copy, silu=silu, weighted_hi=weighted_hi,
                         y_copy=y_copy)
            for step, b, i in steps_of(SCALAR_STEPS):
                parts[step](b, i)

        @block.vector
        def _(dve):
            v = nc.vector
            steps = [0]

            def mark(ins):
                steps[0] += 1
                ins.then_inc(dve_step, 1)

            def link(ins):
                mark(ins)
                dve.wait_ge(dve_step, steps[0])

            root_step = {}

            def row_stats(stage, b, t, src):
                v.bn_stats(stats[:, stage, b, t, :], src[:, t, :]).then_inc(stat_ready[b], 1)

            def reciprocal_root(stage, b, n):
                var, half, root = ln_var[:, stage, b], ln_half[:, stage, b], ln_root[:, stage, :, b]
                if n > 0:
                    dve.wait_ge(dve_step, root_step[stage, str(b)])
                if n == 0:
                    mark(v.tensor_scalar(var, meanvar[:, stage, b, :, 1], EPS, None, ALU.add))
                elif n == 1:
                    mark(v.tensor_scalar(half, var.bitcast(i32), 1, None, ALU.arith_shift_right))
                elif n == 2:
                    mark(v.tensor_scalar(root[:, 0], half, -1.0, float(0x5f3759df), ALU.mult, ALU.add))
                else:
                    k, part = (n - 3) // 3, (n - 3) % 3
                    y0, y1 = root[:, k].bitcast(f32), root[:, k + 1].bitcast(f32)
                    h0, h1 = ln_tmp[:, stage, 2 * k, b], ln_tmp[:, stage, 2 * k + 1, b]
                    if part == 0:
                        mark(v.scalar_tensor_tensor(h0, y0, -0.5, y0, ALU.mult, ALU.mult))
                    elif part == 1:
                        mark(v.tensor_tensor(h1, h0, var, ALU.mult))
                    else:
                        mark(v.scalar_tensor_tensor(y1, h1, 1.5, y0, ALU.add, ALU.mult))
                root_step[stage, str(b)] = steps[0]

            def row_aggregates(stage, b):
                dve.wait_ge(stat_ready[b], 2 * NT * stage + NT)
                for t in range(NT):
                    v.bn_aggr(meanvar[:, stage, b, t, :], stats[:, stage, b, t, :]).then_inc(stat_ready[b], 1)
                dve.wait_ge(stat_ready[b], 2 * NT * (stage + 1))

            def normalise(stage, b, src):
                dve.wait_ge(dve_step, root_step[stage, str(b if stage else slice(0, B))])
                if stage > 0:
                    dve.wait_ge(norm_T_mm[b], stage)
                for t in range(NT):
                    v.tensor_scalar(xn[b][:, t, :], src[:, t, :], meanvar[:, stage, b, t, 0:1],
                                    ln_root[:, stage, 3, b, t:t + 1].bitcast(f32), ALU.subtract,
                                    ALU.mult).then_inc(norm_ready[b], 1)

            def norm1(b, part):
                if part == 0:
                    for n in range(B):
                        dve.wait_ge(d_x[n], 16)
                        for t in range(NT):
                            row_stats(0, n, t, x_sb[n])
                    for n in range(B):
                        row_aggregates(0, n)
                    for n in range(ROOT_OPS):
                        reciprocal_root(0, slice(0, B), n)
                else:
                    normalise(0, b, x_sb[b])

            def norm2(b, part):
                if part == 0:
                    row_aggregates(1, b)
                elif part <= ROOT_OPS:
                    reciprocal_root(1, b, part - 1)
                else:
                    normalise(1, b, x1[b])

            def norm3(b, part):
                if part == 0:
                    dve.wait_ge(x2_ready[b], 1)
                    for t in range(NT):
                        row_stats(2, b, t, x2[b])
                    row_aggregates(2, b)
                elif part <= ROOT_OPS:
                    reciprocal_root(2, b, part - 1)
                else:
                    normalise(2, b, x2[b])

            def val_copy(b, _):
                dve.wait_ge(v_mm[b], 1)
                v.tensor_copy(val[b][:, :, :], U[b][:, :].rearrange("p (t d) -> p t d", d=D)
                              ).then_inc(v_ready[b], 1)

            def keys_full(b, _):
                dve.wait_ge(d_cross, 16)
                dve.wait_ge(k_mm[b], 1)
                v.tensor_tensor(k_full[b][:, :, :], W[b][0:QR, 0:GK].rearrange("p (j t) -> p j t", j=NG),
                                crossw[0:QR, X_BK:X_BK + NG].unsqueeze(2).broadcast_to([QR, NG, TC]),
                                ALU.add).then_inc(k_full_ready[b], 1)

            def keys_lo(b, _):
                dve.wait_ge(k_hi[b], 1)
                v.tensor_tensor(r(k_split[b][2 * GR:QR, :, :]), k_full[b][2 * GR:QR, :, :],
                                k_split[b][2 * GR:QR, :, :], ALU.subtract).then_inc(k_lo[b], 1)

            def value_rows(b, _):
                dve.wait_ge(d_cross, 16)
                dve.wait_ge(v2_mm[b], 1)
                for c in range(NC):
                    k = CROWS[c]
                    v.tensor_tensor(v_rows[b][0:k, c, :], V[b][0:k, c * D:(c + 1) * D],
                                    crossw[0:k, X_BV:X_BV + D], ALU.add).then_inc(v2_rows[b], 1)

            def rowmax1(b, n):
                i = NT - 1 - n
                dve.wait_ge(s_mm[b], n + 1)
                v.tensor_reduce(negmax[:, b, i:i + 1], (V, U)[n % 2][b][:, 0:(i + 1) * P], AX.X, ALU.max,
                                negate=True).then_inc(s_max[b], 1)

            def rowinv(b, n):
                i = NT - 1 - n
                dve.wait_ge(p_ready[b], n + 1)
                v.reciprocal(rowinv_sb[:, b, i:i + 1], rowsum[:, b, i:i + 1]).then_inc(inv_ready[b], 1)

            def residual1(b, n):
                i = NT - 1 - n
                dve.wait_ge(inv_ready[b], n + 1)
                dve.wait_ge(o_mm[b], n + 1)
                v.scalar_tensor_tensor(x1[b][:, i, :], T[b][:, i * P:(i + 1) * P],
                                       rowinv_sb[:, b, i:i + 1], x_sb[b][:, i, :], ALU.mult,
                                       ALU.add).then_inc(x1_ready[b], 1)

            def stats1(b, n):
                dve.wait_ge(x1_ready[b], n + 1)
                row_stats(1, b, NT - 1 - n, x1[b])

            def query_lo(b, j):
                dve.wait_ge(q_hi[b], j + 1)
                v.scalar_tensor_tensor(r(q_split[b][j][GR:2 * GR, :]),
                                       (V, W)[vw_use["query", b, j] % 2][b][GR:2 * GR, :],
                                       crossw[GR:2 * GR, X_BQ + j:X_BQ + j + 1],
                                       q_split[b][j][GR:2 * GR, :], ALU.add, ALU.subtract
                                       ).then_inc(vw_read[b], 1)

            def rowmax2(b, at):
                n, j, i = vw_use["scores2", b, at], at // NT, at % NT
                dve.wait_ge(s2_mm[b], at + 1)
                v.tensor_reduce(max2[:, b, j, i, :],
                                (V, W)[n % 2][b][:, 0:GK].rearrange("p (h t) -> p h t", h=HG), AX.X,
                                ALU.max, negate=True).then_inc(vw_read[b], 1)

            def max_split(b, j):
                dve.wait_ge(vw_read[b], vw_use["scores2", b, NT * j + NT - 1] + 1)
                hi, lo = max2_split[:, b, j, :, 0:HG], max2_split[:, b, j, :, HG:MR]
                link(v.tensor_copy(r(hi), max2[:, b, j, :, :]))
                v.tensor_tensor(r(lo), max2[:, b, j, :, :], hi, ALU.subtract).then_inc(m_split[b], 1)

            def den_inverse(b, _):
                dve.wait_ge(dT_mm[b], 1)
                link(v.reciprocal(den_inv[:, b, :, :],
                                  W[b][:, :].rearrange("p (t h d) -> p t h d", t=NT, d=HD)[:, :, :, 0]))
                v.tensor_copy(den_inv8[b][:, :, :].rearrange("p t (h d) -> p t h d", d=HD),
                              den_inv[:, b, :, :].unsqueeze(3).broadcast_to([P, NT, NH, HD])
                              ).then_inc(dinv_ready[b], 1)

            def y_scale(b, _):
                dve.wait_ge(rT_mm[b], 1)
                dve.wait_ge(sums_ready[b], 2)
                v.tensor_tensor(yT[b][:, :], num_sb[b][:, :], W[b][:, :], ALU.mult).then_inc(yT_ready[b], 1)

            def residual2(b, _):
                dve.wait_ge(wp_mm[b], 1)
                dve.wait_ge(x1b_ready[b], 1)
                v.tensor_tensor(x2[b][:, :, :], x1b[b][:, :, :],
                                V[b][:, :].rearrange("p (t d) -> p t d", d=D), ALU.add).then_inc(x2_ready[b], 1)

            def t_lo(b, _):
                dve.wait_ge(tT_hi_ready[b], 1)
                v.tensor_tensor(r(tT_lo[b][:, :]), T[b][:, :], tT_hi[b][:, :],
                                ALU.subtract).then_inc(tT_lo_ready[b], 1)

            def router_gate(b, _):
                dve.wait_ge(rout_tanh[b], 1)
                dve.wait_ge(rout_z[b], 1)
                v.scalar_tensor_tensor(routT[b][:, :], router_th[b][:, :], 1.0, router_z[b][:, :], ALU.add,
                                       ALU.mult).then_inc(rout_ready[b], 1)

            def top2(b, part):
                lg = logits[:, b]
                if part == 0:
                    dve.wait_ge(d_ffn, 16)
                    dve.wait_ge(lg_mm[b], 1)
                    link(v.scalar_tensor_tensor(
                        lg, V[b][:, 0:NT * NE].rearrange("p (t e) -> p t e", e=NE), 0.5,
                        ffnw[:, F_RB2:F_RB2 + NE].unsqueeze(1).broadcast_to([P, NT, NE]), ALU.mult, ALU.add))
                    for t in range(NT):
                        mark(v.max(top8[:, b, t, :], lg[:, t, :]))
                    dve.wait_ge(dve_step, steps[0])
                    v.tensor_tensor(gap[:, b, :], top8[:, b, :, 1], top8[:, b, :, 0],
                                    ALU.subtract).then_inc(gap_ready[b], 1)
                    for t in range(NT):
                        mark(v.max_index(top8_at[:, b, t, :], top8[:, b, t, :], lg[:, t, :]))
                    dve.wait_ge(dve_step, steps[0])
                    mark(v.tensor_copy(top_at[:, b, :, :], top8_at[:, b, :, 0:TOPK]))
                    return
                dve.wait_ge(dve_step, steps[0])
                for k in range(TOPK):
                    mark(v.tensor_tensor(w_hot[:, b, k], cst[:, C_IOTA:C_IOTA + NE].unsqueeze(1)
                                         .broadcast_to([P, NT, NE]),
                                         top_at[:, b, :, k].unsqueeze(2).broadcast_to([P, NT, NE]),
                                         ALU.is_equal))
                dve.wait_ge(tanh_ready[b], 1)
                for k in range(TOPK):
                    mark(v.tensor_scalar(w_top[:, b, k, :], gap_tanh[:, b, :], (-0.5, 0.5)[k], 0.5,
                                         ALU.mult, ALU.add))
                dve.wait_ge(dve_step, steps[0])
                for k in range(TOPK):
                    mark(v.tensor_tensor(w_part[:, b, k], w_hot[:, b, k],
                                         w_top[:, b, k, :].unsqueeze(2).broadcast_to([P, NT, NE]), ALU.mult))
                dve.wait_ge(dve_step, steps[0])
                v.tensor_tensor(w_all[:, b], w_part[:, b, 0], w_part[:, b, 1], ALU.add).then_inc(w_ready[b], 1)

            def weights_split(b, _):
                dve.wait_ge(wT_full[b], 1)
                v.tensor_copy(r(wT_split[b][0:NE, :]), V[b][0:NE, :]).then_inc(wT_ready[b], 1)
                dve.wait_ge(wT_ready[b], 1)
                v.tensor_tensor(r(wT_split[b][32:32 + NE, :]), V[b][0:NE, :], wT_split[b][0:NE, :],
                                ALU.subtract).then_inc(wT_ready[b], 1)

            def scale(b, u):
                dve.wait_ge(silu_ready[b], u + 1)
                dve.wait_ge(wb_mm[b], u // FC + 1)
                h = hid[b][u % NHID][:, :]
                v.tensor_tensor(h, h, V[b][:, :], ALU.mult).then_inc(hidw_ready[b], 1)

            def weighted_lo(b, u):
                dve.wait_ge(hidw_hi_ready[b], u + 1)
                v.tensor_tensor(r(hidw_lo[b][u % NS][:, :]), hid[b][u % NHID][:, :], hidw_hi[b][u % NS][:, :],
                                ALU.subtract).then_inc(hidw_lo_ready[b], 1)

            def add_rows(b, half):
                dve.wait_ge(yo_mm[b], half + 1)
                dve.wait_ge(res_ready[b], 1)
                at = slice(half * NT // 2, (half + 1) * NT // 2)
                v.tensor_tensor(out_sb[b][:, at, :], res[b][:, at, :], (T, U)[half][b][:, :]
                                .rearrange("p (t d) -> p t d", d=D)[:, at, :], ALU.add).then_inc(out_ready[b], 1)

            parts = dict(norm1=norm1, norm2=norm2, norm3=norm3, val_copy=val_copy, keys_full=keys_full, keys_lo=keys_lo,
                         value_rows=value_rows, rowmax1=rowmax1, rowinv=rowinv, residual1=residual1,
                         stats1=stats1, query_lo=query_lo, rowmax2=rowmax2, max_split=max_split,
                         den_inverse=den_inverse, y_scale=y_scale, residual2=residual2, t_lo=t_lo, router_gate=router_gate,
                         top2=top2, weights_split=weights_split, scale=scale, weighted_lo=weighted_lo,
                         add_rows=add_rows)
            for step, b, i in steps_of(VECTOR_STEPS):
                parts[step](b, i)

        @block.tensor
        def _(pe):
            mm, tr = nc.tensor.matmul, nc.tensor.transpose

            def cols(i):
                return slice(i * P, (i + 1) * P)

            pe.wait_ge(d_self, 16)
            mm(T[1][:, 0:P], selfw[:, 0:P], selfw[:, P:2 * P], start=True, stop=True)
            mm(T[1][:, P:2 * P], selfw[:, 2 * P:3 * P], selfw[:, 3 * P:4 * P], start=True,
               stop=True).then_inc(aw_mm, 1)
            pe.wait_ge(d_const, 16)

            def x_T(b, stage):
                if stage == 0 and b == 1:
                    pe.wait_ge(aw_ready, 2)
                if stage == 1:
                    pe.wait_ge(x1_ready[b], NT)
                for t in range(NT):
                    pe.wait_ge(norm_ready[b], NT * stage + t + 1)
                    last = tr(T[b][:, cols(t)], xn[b][:, t, :], ident)
                last.then_inc(norm_T_mm[b], 1)

            def context_T(b, _):
                pe.wait_ge(d_ctx, 16)
                for n in range(B):
                    last = tr(W[0][:, n * TC:(n + 1) * TC], ctx_sb[:, n, :], ident[0:TC, 0:TC])
                last.then_inc(ctxT_mm, 1)

            def project1(b, _):
                pe.wait_ge(aw_ready, 2)
                pe.wait_ge(norm_T_ready[b], 1)
                mm(T[b][:, :], a_sb[:, :], xT[b][:, :], start=True, stop=True).then_inc(g_mm[b], 1)
                for t in range(NT):
                    last = mm(U[b][:, cols(t)], xT[b][:, cols(t)], w12[:, :], start=True, stop=True)
                last.then_inc(v_mm[b], 1)

            def keys(b, _):
                pe.wait_ge(d_cross, 16)
                pe.wait_ge(ctxT_ready, B)
                for j in range(NG):
                    last = mm(W[b][0:QR, j * TC:(j + 1) * TC], crossw[:, X_WK + j * QR:X_WK + (j + 1) * QR],
                              ctxT[:, b, 0, :], start=True, stop=True)
                last.then_inc(k_mm[b], 1)

            def values(b, _):
                flat = ctxT[:, b, :, :].rearrange("p h t -> p (h t)")
                for c in range(NC):
                    last = mm(V[b][0:CROWS[c], cols(c)], flat[:, c * CR:c * CR + CROWS[c]],
                              crossw[:, X_WV:X_WV + D], start=True, stop=True)
                last.then_inc(v2_mm[b], 1)

            def scores1(b, n):
                i = NT - 1 - n
                if n == 0:
                    pe.wait_ge(mask_ready, 2)
                    pe.wait_ge(g_ready[b], 1)
                    pe.wait_ge(v2_rows[b], NC)
                elif n == 1:
                    pe.wait_ge(v_ready[b], 1)
                else:
                    pe.wait_ge(p_ready[b], n - 1)
                sc = (V, U)[n % 2][b]
                mm(sc[:, 0:(i + 1) * P], gT[b][:, cols(i)], xT[b][:, 0:(i + 1) * P], start=True, stop=False)
                mm(sc[:, cols(i)], ident_b[:, :], causal_b[:, :], start=False, stop=True).then_inc(s_mm[b], 1)

            def probs_T(b, n):
                i = NT - 1 - n
                pe.wait_ge(p_ready[b], n + 1)
                if n > 0:
                    pe.wait_ge(pT_ready[b], n)
                else:
                    pe.wait_ge(k_full_ready[b], 1)
                for k in range(i + 1):
                    last = tr(W[b][:, cols(k)], prob[b][i][:, cols(k)], ident)
                last.then_inc(pT_mm[b], 1)

            def attend1(b, n):
                i = NT - 1 - n
                if n == 0:
                    pe.wait_ge(g_ready[b], 1)
                else:
                    pe.wait_ge(x1_ready[b], n)
                pe.wait_ge(pT_ready[b], n + 1)
                for k in range(i + 1):
                    last = mm(T[b][:, cols(i)], probT[b][i][:, cols(k)], val[b][:, k, :],
                              start=(k == 0), stop=(k == i))
                last.then_inc(o_mm[b], 1)

            def query(b, j):
                n = vw_use["query", b, j]
                if n >= 2:
                    pe.wait_ge(vw_read[b], n - 1)
                elif n == 0:
                    pe.wait_ge(p_ready[b], NT)
                    pe.wait_ge(norm_T_ready[b], 2)
                else:
                    pe.wait_ge(pT_ready[b], NT)
                mm((V, W)[n % 2][b][0:QR, :], crossw[:, X_WQ + j * QR:X_WQ + (j + 1) * QR], xT[b][:, :],
                   start=True, stop=True).then_inc(q_mm[b], 1)

            def scores2(b, at):
                n, j, i = vw_use["scores2", b, at], at // NT, at % NT
                pe.wait_ge(vw_read[b], vw_use["query", b, j] + 1)
                pe.wait_ge(vw_read[b], n - 1)
                pe.wait_ge(k_ready[b], j + 1)
                mm((V, W)[n % 2][b][:, 0:GK], r(q_split[b][j][0:QR, cols(i)]), r(k_diag[b][0:QR, j, :]),
                   start=True, stop=True).then_inc(s2_mm[b], 1)

            def maxima_T(b, j):
                n = tu_use["maxima_T", b, j]
                pe.wait_ge(m_split[b], j + 1)
                if n >= 3:
                    pe.wait_ge(tu_read[b], n - 2)
                for i in range(NT):
                    last = tr((T, U)[n % 2][b][0:MR, cols(i)], max2_split[:, b, j, i, :], ident)
                last.then_inc(tu_mm[b], 1)

            def keyscores2(b, at):
                n, j, c = tu_use["keyscores2", b, at], at // NC, at % NC
                if n >= 3:
                    pe.wait_ge(tu_read[b], n - 2)
                pe.wait_ge(tu_read[b], tu_use["maxima_T", b, j])
                mm((T, U)[n % 2][b][0:CROWS[c], :], r(k_diag[b][:, j, c * CR:c * CR + CROWS[c]]),
                   r(q_split[b][j][0:QR + MR, :]), start=True, stop=True).then_inc(tu_mm[b], 1)

            def attend2(b, part):
                c, dst = part % NC, (W, V)[part // NC]
                if part == 0:
                    pe.wait_ge(ones_ready, 1)
                    pe.wait_ge(vw_read[b], NG + NG * NT)
                    pe.wait_ge(tu_read[b], NG + NG * NC)
                if part == NC:
                    pe.wait_ge(v2_ready[b], NC)
                k = CROWS[c]
                for j in range(NG):
                    lhsT = v_diag[b][0:k, c, j * GR:(j + 1) * GR] if dst is V else ones_diag[0:k, c, :]
                    last = mm(dst[b][j * GR:(j + 1) * GR, :], lhsT, prob2[b][j * NC + c][0:k, :],
                              start=(c == 0), stop=(c == NC - 1), tile_position=(0, j * GR))
                if c == NC - 1:
                    last.then_inc(sums_mm[b], 1)

            def den_T(b, _):
                pe.wait_ge(sums_ready[b], 1)
                for i in range(NT):
                    last = tr(W[b][:, cols(i)], den_sb[b][:, cols(i)], ident)
                last.then_inc(dT_mm[b], 1)

            def den_back(b, _):
                pe.wait_ge(dinv_ready[b], 1)
                for i in range(NT):
                    last = tr(W[b][:, cols(i)], den_inv8[b][:, i, :], ident)
                last.then_inc(rT_mm[b], 1)

            def project(b, _):
                pe.wait_ge(yT_ready[b], 1)
                for i in range(NT):
                    last = mm(V[b][:, cols(i)], yT[b][:, cols(i)], crossw[:, X_WP:X_WP + D], start=True,
                              stop=True)
                last.then_inc(wp_mm[b], 1)

            def router(b, _):
                pe.wait_ge(d_ffn, 16)
                pe.wait_ge(norm_T_ready[b], 3)
                mm(U[b][:, :], ffnw[:, F_RW1:F_RW1 + P], tT[b][:, :], start=True, stop=True).then_inc(hid_mm[b], 1)

            def logits_(b, _):
                pe.wait_ge(rout_ready[b], 1)
                pe.wait_ge(x2_ready[b], 1)
                for t in range(NT):
                    last = mm(V[b][:, t * NE:(t + 1) * NE], routT[b][:, cols(t)], ffnw[:, F_RW2:F_RW2 + NE],
                              start=True, stop=True)
                last.then_inc(lg_mm[b], 1)

            def weights_T(b, _):
                pe.wait_ge(w_ready[b], 1)
                for t in range(NT):
                    last = tr(V[b][0:NE, cols(t)], w_all[:, b, t, :], ident)
                last.then_inc(wT_mm[b], 1)

            def hidden(b, u):
                e, c = u // FC, u % FC
                h = slice(c * P, (c + 1) * P)
                if u == 0:
                    pe.wait_ge(tT_lo_ready[b], 1)
                elif u == 1:
                    pe.wait_ge(rout_z[b], 1)
                else:
                    pe.wait_ge(silu_ready[b], u - 1)
                pe.wait_ge(w1_ready, e + 1)
                z = (T, U)[u % 2][b][:, :]
                mm(z, r(w1_hi[:, e, h]), r(tT_hi[b][:, :]), start=True, stop=False)
                mm(z, r(w1_lo[:, e, h]), r(tT_hi[b][:, :]), start=False, stop=False)
                mm(z, r(w1_hi[:, e, h]), r(tT_lo[b][:, :]), start=False, stop=True).then_inc(z_mm[b], 1)

            def weight_row(b, e):
                if e == 0:
                    pe.wait_ge(pick_ready, 1)
                    pe.wait_ge(wT_ready[b], 2)
                    pe.wait_ge(d_eb2, 16)
                    mm(W[b][:, :], eb2_sb[:, :], wT[b][0:NE, :], start=True, stop=False)
                else:
                    pe.wait_ge(hidw_ready[b], FC * e)
                mm(V[b][:, :], r(pick[:, e:e + 1]).broadcast_to([32 + NE, P]), r(wT_split[b][:, :]), start=True,
                   stop=True).then_inc(wb_mm[b], 1)

            def expert(b, u):
                e, c = u // FC, u % FC
                at = slice((u % (EPB * FC)) * D, (u % (EPB * FC) + 1) * D)
                w_hi, w_lo = r(w2_hi[e // EPB][:, at]), r(w2_lo[e // EPB][:, at])
                h_hi, h_lo = r(hidw_hi[b][u % NS][:, :]), r(hidw_lo[b][u % NS][:, :])
                pe.wait_ge(w2_ready, e + 1)
                pe.wait_ge(hidw_hi_ready[b], u + 1)
                mm(W[b][:, :], w_hi, h_hi, start=False, stop=False)
                mm(W[b][:, :], w_lo, h_hi, start=False, stop=False)
                pe.wait_ge(*lo_done(b, u))
                mm(W[b][:, :], w_hi, h_lo, start=False, stop=(u == NU - 1)).then_inc(e_mm[b], 1)

            def finish(b, half):
                for i in (2 * half, 2 * half + 1):
                    pe.wait_ge(y_ready[b], half + 1)
                    last = tr((T, U)[half][b][:, cols(i)], y_sb[b][:, cols(i)], ident)
                last.then_inc(yo_mm[b], 1)

            parts = dict(x_T=x_T, t_T=x_T, context_T=context_T, project1=project1, keys=keys,
                         values=values, scores1=scores1, probs_T=probs_T, attend1=attend1, query=query,
                         scores2=scores2, maxima_T=maxima_T, keyscores2=keyscores2, attend2=attend2,
                         den_T=den_T, den_back=den_back, project=project, router=router, logits=logits_,
                         weights_T=weights_T, hidden=hidden, weight_row=weight_row, expert=expert,
                         finish=finish)
            for step, b, i in steps_of(TENSOR_STEPS):
                parts[step](b, i)


def kernel(**inputs):
    import numpy as np
    import concourse.bacc as bacc
    from concourse.bass_utils import run_bass_kernel_spmd

    a = {k: np.ascontiguousarray(v) for k, v in inputs.items()}
    row = np.arange(P)
    causal = np.where(row[None, :] > row[:, None], MASKED, 0.0)
    hrow = np.where(row < QR, (row % GR) // HD, (row - QR) % HG)
    hmask = hrow[:, None] == np.arange(HG)[None, :]
    pair = np.arange(NC)[None, :] * CR + row[:, None]
    vmask = ((pair // TC)[:, :, None] == np.arange(HG)[None, None, :]).reshape(P, NC * HG)
    iota = np.tile(np.arange(NE)[None, :], (P, 1))
    pick = (row % 32)[:, None] == np.arange(NE)[None, :]
    consts = np.concatenate([np.eye(P), causal, hmask, vmask, iota, pick], 1).astype(np.float32)

    def rep(w):
        parts = [w[..., j * GR:(j + 1) * GR] for j in range(NG) for _ in range(REPS)]
        return np.concatenate(parts, -1)

    def across(v):
        return np.tile(v[None, :], (P, 1))

    self_w = np.concatenate([a["L0_attn_w_q"].T, a["L0_attn_w_k"].T, a["L0_attn_w_v1"].T,
                             a["L0_attn_w_v2"]], 1)
    bq, bk = (np.concatenate([rep(a[n]).reshape(NG, QR).T, np.zeros((P - QR, NG), np.float32)], 0)
              for n in ("L0_xattn_bq", "L0_xattn_bk"))
    cross_w = np.concatenate([rep(a["L0_xattn_Wq"].T), rep(a["L0_xattn_Wk"].T), a["L0_xattn_Wv"].T,
                              a["L0_xattn_Wp"].T, bq, across(a["L0_xattn_bv"]), across(a["L0_xattn_bp"]),
                              bk], 1)
    ffn_w = np.concatenate([a["L0_ffn_rw1"], a["L0_ffn_rw2"], a["L0_ffn_rb1"][:, None],
                            a["L0_ffn_eb1"].reshape(NU, P).T, across(a["L0_ffn_rb2"])], 1)
    arrays = {"x": a["x"], "ctx": a["ctx_1024"], "consts": consts, "self_w": self_w, "cross_w": cross_w,
              "ffn_w": ffn_w, "eb2": a["L0_ffn_eb2"], "ew1": a["L0_ffn_ew1"],
              "ew2": a["L0_ffn_ew2"]}
    arrays = {k: np.ascontiguousarray(v) for k, v in arrays.items()}
    nc = bacc.Bacc("TRN2", target_bir_lowering=False, num_devices=1)
    aps = [nc.dram_tensor(f"in_{k}", v.shape, mybir.dt.float32, kind="ExternalInput").ap()
           for k, v in arrays.items()]
    out = nc.dram_tensor("out", (B, S, D), mybir.dt.float32, kind="ExternalOutput").ap()
    decoder_block(nc, *aps, out)
    result = run_bass_kernel_spmd(nc, [{f"in_{k}": v for k, v in arrays.items()}], core_ids=[0])
    return result.results[0]["out"]
```
